# Optimizing a Trainium2 kernel written in Bass

```python
import numpy as np
import jax
import jax.numpy as jnp

def _softmax(x, axis=-1):
    return jax.nn.softmax(x, axis=axis)

def _gelu(x):
    return jax.nn.gelu(x, approximate=True)

def _silu(x):
    return jax.nn.silu(x)

def _sigmoid(x):
    return jax.nn.sigmoid(x)

def _layernorm(x, axis=-1, eps=1e-05):
    m = jnp.mean(x, axis=axis, keepdims=True)
    v = jnp.var(x, axis=axis, keepdims=True)
    return (x - m) / jnp.sqrt(v + eps)

def _scatter_add(tgt, idx, src, axis=0):
    return tgt.at[idx].add(src)

def _segment_sum(src, seg, n):
    return jax.ops.segment_sum(src, seg, n)
kernel_name = 'mk_pixart_seq_d1_seqx_r4_6361f2'

def setup_inputs(seed: int=0):
    np.random.seed(seed)
    _w = jnp.asarray

    def _rec_inputs():
        import jax
        import jax.numpy as jnp
        _rk = jax.random.key(seed)
        x = -0.0002928 + 1 * jax.random.normal(jax.random.fold_in(_rk, 1), (32, 256, 256), jnp.float32)
        _lenS = 256 - jax.random.randint(jax.random.fold_in(_rk, 7), (32,), 0, max(1, 256 // 4) + 1, jnp.int32)
        _lenS2 = 77 - jax.random.randint(jax.random.fold_in(_rk, 8), (32,), 0, max(1, 77 // 4) + 1, jnp.int32)
        cond_1024 = 0.000887014 + 1.03683 * jax.random.normal(jax.random.fold_in(_rk, 11), (32, 256), jnp.float32)
        _ctx_1024P = jax.random.normal(jax.random.fold_in(_rk, 12), (32, 16, 256), jnp.float32)
        _ctx_1024c = jax.random.dirichlet(jax.random.fold_in(_rk, 512), 0.3 * jnp.ones((16,), jnp.float32), (32, 77))
        _ctx_1024t = jnp.einsum('bsk,bkd->bsd', _ctx_1024c, _ctx_1024P)
        _ctx_1024t = _ctx_1024t * jax.lax.rsqrt(jnp.mean(jnp.square(_ctx_1024t)) + 1e-12) * 0.953939
        ctx_1024 = 0.00086875 + 0.999764 * (_ctx_1024t + 0.3 * jax.random.normal(jax.random.fold_in(_rk, 612), (32, 77, 256), jnp.float32))
        return (x, cond_1024, ctx_1024)
    x, cond_1024, ctx_1024 = _rec_inputs()

    def _L0_xcond_setup():
        import jax, jax.numpy as jnp
        import numpy as np
        import math
        D_MODEL = 256
        N_HEADS = 16
        HEAD_DIM = D_MODEL // N_HEADS
        D_FF = 1024
        EPS = 1e-05
        ROPE_BASE = 10000.0

        def _rope(t):
            L, Dh = (t.shape[1], t.shape[-1])
            half = Dh // 2
            inv_freq = 1.0 / ROPE_BASE ** (jnp.arange(half, dtype=t.dtype) / half)
            ang = jnp.arange(L, dtype=t.dtype)[:, None] * inv_freq[None, :]
            cos = jnp.cos(ang)[None, :, None, :]
            sin = jnp.sin(ang)[None, :, None, :]
            t1, t2 = (t[..., :half], t[..., half:])
            return jnp.concatenate([t1 * cos - t2 * sin, t2 * cos + t1 * sin], axis=-1)

        def _adaln(x, emb, w, b):
            e = emb[:, 0, :]
            gb = e @ w.T + b
            gamma, beta = jnp.split(gb, 2, axis=-1)
            mu = x.mean(-1, keepdims=True)
            var = x.var(-1, keepdims=True)
            xn = (x - mu) * jax.lax.rsqrt(var + EPS)
            return xn * (1.0 + gamma[:, None, :]) + beta[:, None, :]

        def _attn(q, k, v):
            scale = 1.0 / math.sqrt(HEAD_DIM)
            scores = jnp.einsum('bqhd,bkhd->bhqk', q, k) * scale
            w = jax.nn.softmax(scores, axis=-1)
            out = jnp.einsum('bhqk,bkhd->bqhd', w, v)
            B, Lq = (out.shape[0], out.shape[1])
            return out.reshape(B, Lq, D_MODEL)
        key = jax.random.key(seed)
        ks = jax.random.split(key, 24)
        s = 0.02
        inp = {'x': jax.random.normal(ks[0], (2, 512, D_MODEL), jnp.float32), 'noise_emb': jax.random.normal(ks[1], (2, 1, D_MODEL), jnp.float32), 'context': jax.random.normal(ks[2], (2, 256, D_MODEL), jnp.float32), 'ln1_w': jax.random.normal(ks[3], (2 * D_MODEL, D_MODEL), jnp.float32) * s, 'ln1_b': jax.random.normal(ks[4], (2 * D_MODEL,), jnp.float32) * s, 'ln2_w': jax.random.normal(ks[5], (2 * D_MODEL, D_MODEL), jnp.float32) * s, 'ln2_b': jax.random.normal(ks[6], (2 * D_MODEL,), jnp.float32) * s, 'ln3_w': jax.random.normal(ks[7], (2 * D_MODEL, D_MODEL), jnp.float32) * s, 'ln3_b': jax.random.normal(ks[8], (2 * D_MODEL,), jnp.float32) * s, 'qkv_w': jax.random.normal(ks[9], (3 * D_MODEL, D_MODEL), jnp.float32) * s, 'sa_out_w': jax.random.normal(ks[10], (D_MODEL, D_MODEL), jnp.float32) * s, 'q_w': jax.random.normal(ks[11], (D_MODEL, D_MODEL), jnp.float32) * s, 'k_w': jax.random.normal(ks[12], (D_MODEL, D_MODEL), jnp.float32) * s, 'v_w': jax.random.normal(ks[13], (D_MODEL, D_MODEL), jnp.float32) * s, 'ca_out_w': jax.random.normal(ks[14], (D_MODEL, D_MODEL), jnp.float32) * s, 'ffn_w1': jax.random.normal(ks[15], (D_FF, D_MODEL), jnp.float32) * s, 'ffn_b1': jax.random.normal(ks[16], (D_FF,), jnp.float32) * s, 'ffn_w2': jax.random.normal(ks[17], (D_MODEL, D_FF), jnp.float32) * s, 'ffn_b2': jax.random.normal(ks[18], (D_MODEL,), jnp.float32) * s}
        return inp
    _L0_xcond_all = _L0_xcond_setup()
    _L0_xcond_in = {k: v for k, v in _L0_xcond_all.items() if k in ('ln1_w', 'ln1_b', 'ln2_w', 'ln2_b', 'ln3_w', 'ln3_b', 'qkv_w', 'sa_out_w', 'q_w', 'k_w', 'v_w', 'ca_out_w', 'ffn_w1', 'ffn_b1', 'ffn_w2', 'ffn_b2')}
    del _L0_xcond_all
    return {'x': x, 'cond_1024': cond_1024, 'ctx_1024': ctx_1024, 'L0_xcond_ln1_w': _L0_xcond_in['ln1_w'], 'L0_xcond_ln1_b': _L0_xcond_in['ln1_b'], 'L0_xcond_ln2_w': _L0_xcond_in['ln2_w'], 'L0_xcond_ln2_b': _L0_xcond_in['ln2_b'], 'L0_xcond_ln3_w': _L0_xcond_in['ln3_w'], 'L0_xcond_ln3_b': _L0_xcond_in['ln3_b'], 'L0_xcond_qkv_w': _L0_xcond_in['qkv_w'], 'L0_xcond_sa_out_w': _L0_xcond_in['sa_out_w'], 'L0_xcond_q_w': _L0_xcond_in['q_w'], 'L0_xcond_k_w': _L0_xcond_in['k_w'], 'L0_xcond_v_w': _L0_xcond_in['v_w'], 'L0_xcond_ca_out_w': _L0_xcond_in['ca_out_w'], 'L0_xcond_ffn_w1': _L0_xcond_in['ffn_w1'], 'L0_xcond_ffn_b1': _L0_xcond_in['ffn_b1'], 'L0_xcond_ffn_w2': _L0_xcond_in['ffn_w2'], 'L0_xcond_ffn_b2': _L0_xcond_in['ffn_b2']}

def reference(x, cond_1024, ctx_1024, L0_xcond_ln1_w, L0_xcond_ln1_b, L0_xcond_ln2_w, L0_xcond_ln2_b, L0_xcond_ln3_w, L0_xcond_ln3_b, L0_xcond_qkv_w, L0_xcond_sa_out_w, L0_xcond_q_w, L0_xcond_k_w, L0_xcond_v_w, L0_xcond_ca_out_w, L0_xcond_ffn_w1, L0_xcond_ffn_b1, L0_xcond_ffn_w2, L0_xcond_ffn_b2):
    import jax
    import jax.numpy as jnp

    def _L0_xcond_ref(x, noise_emb, context, ln1_w, ln1_b, ln2_w, ln2_b, ln3_w, ln3_b, qkv_w, sa_out_w, q_w, k_w, v_w, ca_out_w, ffn_w1, ffn_b1, ffn_w2, ffn_b2):
        import jax, jax.numpy as jnp
        import numpy as np
        import math
        D_MODEL = 256
        N_HEADS = 16
        HEAD_DIM = D_MODEL // N_HEADS
        D_FF = 1024
        EPS = 1e-05
        ROPE_BASE = 10000.0

        def _rope(t):
            L, Dh = (t.shape[1], t.shape[-1])
            half = Dh // 2
            inv_freq = 1.0 / ROPE_BASE ** (jnp.arange(half, dtype=t.dtype) / half)
            ang = jnp.arange(L, dtype=t.dtype)[:, None] * inv_freq[None, :]
            cos = jnp.cos(ang)[None, :, None, :]
            sin = jnp.sin(ang)[None, :, None, :]
            t1, t2 = (t[..., :half], t[..., half:])
            return jnp.concatenate([t1 * cos - t2 * sin, t2 * cos + t1 * sin], axis=-1)

        def _adaln(x, emb, w, b):
            e = emb[:, 0, :]
            gb = e @ w.T + b
            gamma, beta = jnp.split(gb, 2, axis=-1)
            mu = x.mean(-1, keepdims=True)
            var = x.var(-1, keepdims=True)
            xn = (x - mu) * jax.lax.rsqrt(var + EPS)
            return xn * (1.0 + gamma[:, None, :]) + beta[:, None, :]

        def _attn(q, k, v):
            scale = 1.0 / math.sqrt(HEAD_DIM)
            scores = jnp.einsum('bqhd,bkhd->bhqk', q, k) * scale
            w = jax.nn.softmax(scores, axis=-1)
            out = jnp.einsum('bhqk,bkhd->bqhd', w, v)
            B, Lq = (out.shape[0], out.shape[1])
            return out.reshape(B, Lq, D_MODEL)
        B, L, D = x.shape
        L_ctx = context.shape[1]
        res = x
        xn = _adaln(x, noise_emb, ln1_w, ln1_b)
        qkv = xn @ qkv_w.T
        q, k, v = jnp.split(qkv, 3, axis=-1)
        q = _rope(q.reshape(B, L, N_HEADS, HEAD_DIM))
        k = _rope(k.reshape(B, L, N_HEADS, HEAD_DIM))
        v = v.reshape(B, L, N_HEADS, HEAD_DIM)
        sa = _attn(q, k, v) @ sa_out_w.T
        x = res + sa
        res = x
        xn = _adaln(x, noise_emb, ln2_w, ln2_b)
        q = _rope((xn @ q_w.T).reshape(B, L, N_HEADS, HEAD_DIM))
        k = _rope((context @ k_w.T).reshape(B, L_ctx, N_HEADS, HEAD_DIM))
        v = (context @ v_w.T).reshape(B, L_ctx, N_HEADS, HEAD_DIM)
        ca = _attn(q, k, v) @ ca_out_w.T
        x = res + ca
        res = x
        xn = _adaln(x, noise_emb, ln3_w, ln3_b)
        h = jax.nn.gelu(xn @ ffn_w1.T + ffn_b1, approximate=False)
        x = res + (h @ ffn_w2.T + ffn_b2)
        return x
    x = _L0_xcond_ref(x, cond_1024[:, None, :], ctx_1024, L0_xcond_ln1_w, L0_xcond_ln1_b, L0_xcond_ln2_w, L0_xcond_ln2_b, L0_xcond_ln3_w, L0_xcond_ln3_b, L0_xcond_qkv_w, L0_xcond_sa_out_w, L0_xcond_q_w, L0_xcond_k_w, L0_xcond_v_w, L0_xcond_ca_out_w, L0_xcond_ffn_w1, L0_xcond_ffn_b1, L0_xcond_ffn_w2, L0_xcond_ffn_b2)
    return x

_drawn_inputs = setup_inputs


def setup_inputs(seed=0):
    import zlib

    import numpy as np

    out = dict(_drawn_inputs(seed))
    spreads = {}
    factors = {'L0_xcond_ln1_b': 29.496,
     'L0_xcond_ln2_w': 8.0,
     'L0_xcond_ln2_b': 8.0,
     'L0_xcond_ln3_b': 8.0,
     'L0_xcond_q_w': 8.0,
     'L0_xcond_k_w': 8.0,
     'L0_xcond_ffn_b1': 7.608,
     'L0_xcond_ffn_b2': 2.889}
    for name, (base, spread) in spreads.items():
        noise = np.random.default_rng([zlib.crc32(name.encode()), seed]).standard_normal(out[name].shape)
        drawn = base * np.exp(spread * noise) if base else spread * noise
        out[name] = jnp.asarray(drawn.astype(out[name].dtype))
    for name, factor in factors.items():
        out[name] = (out[name] * factor).astype(out[name].dtype)
    return out
```

```python
from contextlib import ExitStack

import concourse.bass as bass
from concourse import mybir

B, L, D, H, DH, DFF, LC = 32, 256, 256, 16, 16, 1024, 77
P = 128
NT = L // P
NC = D // P
NF = DFF // P
NPAIR = H // 2
SROW = P // 2
NS = 3 * DH
NSM = NS + 2
VW = 32
GRP = P // VW
NG = H // GRP
LCE = LC + LC % 2
EPS = 1e-5
SCALE = 1.0 / DH ** 0.5
A_STACKS = NPAIR
B_STACKS = NPAIR // 2 + 2
A_MAX, B_MAX = NT * NPAIR, NT * NPAIR // 2
A_EXP, B_EXP = H, H // 2
NSLOT = 8
STAGE = {"A": 0, "B": -1, "T": -2, "C": -2}
FIRST_LOOP, END_LOOP = 3, B - 1


class Batch:

    def __init__(self, reg, off):
        self.reg, self.off = reg, off

    def __add__(self, n):
        return Batch(self.reg, self.off + n)

    def times(self, per, k=0):
        c = self.off * per + k
        if self.reg is None:
            return c
        v = self.reg * per if per != 1 else self.reg
        return v + c if c else v


class Event:

    def __init__(self, sem, per, inc, held):
        self.sem, self.per, self.inc, self.held = sem, per, inc, held

    def at(self, batch, k=None):
        if batch.reg is None and batch.off > B - 1:
            batch, k = Batch(None, B - 1), None
        v = batch.times(self.per * self.inc, self.inc * (self.per if k is None else k))
        return self.held if isinstance(v, int) and v <= 0 else (self.sem, v)


class Reuse:

    def __init__(self, held, uses):
        self.held = held
        self.uses = {u[0]: u for u in uses}
        self.last_of_turn = {u[1]: u for u in uses}
        self.last = {}

    def before(self, name, turn):
        _, slot, _, _ = use = self.uses[name]
        end = self.held
        if slot in self.last:
            (_, _, event, k), batch = self.last[slot]
            end = event.at(batch, k)
        self.last[slot] = (use, turn + STAGE[name[0]])
        return end

    def turn_before(self, turn):
        self.last = {s: (u, turn + (STAGE[u[0][0]] - 1)) for s, u in self.last_of_turn.items()}


def run_turns(eng, reuses, body):
    def peeled(t):
        has = {s for s, off in STAGE.items() if 0 <= t + off < B} | ({"N"} if t + 1 < B else set())
        body(Batch(None, t), has)
    for t in range(-1, FIRST_LOOP):
        peeled(t)
    with eng.Fori(FIRST_LOOP, END_LOOP) as i:
        for r in reuses:
            r.turn_before(Batch(i, 0))
        body(Batch(i, 0), set(STAGE) | {"N"})
    for r in reuses:
        r.turn_before(Batch(None, END_LOOP))
    for t in range(END_LOOP, B + 2):
        peeled(t)


def layer_kernel(nc, x, ctx, cond_t, rope, wqkv, wsa, wq, wkv, wca, w1, w2, lnw, lnb, b1, b2, out):
    f32, f32r = mybir.dt.float32, mybir.dt.float32r
    ALU, ACT, AX = mybir.AluOpType, mybir.ActivationFunctionType, mybir.AxisListType
    x_d = x.rearrange("b (t p) d -> b p t d", p=P)
    out_d = out.rearrange("b (t p) d -> b p t d", p=P)

    with ExitStack() as es:
        def sb(name, shape, dt=f32):
            return es.enter_context(nc.sbuf_tensor(name, shape, dt))

        def sem(name):
            return es.enter_context(nc.semaphore(name))

        def event(name, per, inc=1):
            return Event(sem(name), per, inc, HELD)

        names = [("qkv", NC * 3 * D, wqkv), ("sa", NC * D, wsa), ("q", NC * D, wq), ("kv", NC * 2 * D, wkv),
                 ("w1", NC * DFF, w1), ("w2", NF * D, w2), ("ca", NC * D, wca)]
        w_at, total = {}, 0
        for n, cols, _ in names:
            w_at[n] = (total, cols)
            total += cols
        w_hi, w_lo = sb("w_hi", [P, total], f32r), sb("w_lo", [P, total], f32r)

        def weight(name, chunks):
            a, cols = w_at[name]
            return (w_hi[:, a:a + cols].rearrange("p (c n) -> p c n", c=chunks),
                    w_lo[:, a:a + cols].rearrange("p (c n) -> p c n", c=chunks))

        ident, ident_r = sb("ident", [P, P]), sb("ident_r", [P, P], f32r)
        rope_t = sb("rope_t", [P, NT, 3, 8])
        gb = sb("gb", [P, 3, 4, B])
        lnb_t = sb("lnb_t", [P, 12])
        b1_t, b2_t = sb("b1_t", [P, NF]), sb("b2_t", [P, D])
        minus_half = sb("minus_half", [P, NT])
        fence = {s: sb(f"fence_{s}", [P, 1]) for s in "ABC"}
        pool_fence = sb("pool_fence", [P, 32])
        cond_s = sb("cond_s", [P, NC, B])
        x_in, xa, xb, xc = (sb(n, [P, NT, D]) for n in ("x_in", "xa", "xb", "xc"))
        ctx_in = sb("ctx_in", [LC, D])
        xn = {s: sb(f"xn_{s}", [P, NT, D]) for s in "ABC"}
        stats = {s: sb(f"stats_{s}", [P, NT, 6]) for s in "ABC"}
        mv = {s: sb(f"mv_{s}", [P, NT, 2]) for s in "ABC"}
        ve = {s: sb(f"ve_{s}", [P, NT]) for s in "ABC"}
        rstd = {s: sb(f"rstd_{s}", [P, NT]) for s in "ABC"}
        t_f = sb("t_f", [P, NC, L])
        t_hi = {s: sb(f"t_hi_{s}", [P, NC, L], f32r) for s in "ABC"}
        t_lo = {s: sb(f"t_lo_{s}", [P, NC, L], f32r) for s in "ABC"}
        c_hi, c_lo = sb("c_hi", [P, NC, LC], f32r), sb("c_lo", [P, NC, LC], f32r)
        rot_c = sb("rot_c", [P, NT, 2 * D])
        rot_s = sb("rot_s", [P, 2 * D])
        rk_c, rk_s = sb("rk_c", [LC, D]), sb("rk_s", [LC, D])
        q_nat = sb("q_nat", [P, NT, H, SROW], f32r)
        k_nat = sb("k_nat", [P, NT, H, SROW], f32r)
        q_st = {s: sb(f"q_st_{s}", [P, NPAIR, L], f32r) for s in "AB"}
        k_st_a = sb("k_st_a", [P, NPAIR, L], f32r)
        k_st_b = sb("k_st_b", [P, NPAIR, 2, P], f32r)
        v_a = sb("v_a", [P, NT, H, VW])
        v_b = sb("v_b", [LC, H, VW])
        mx = {s: sb(f"mx_{s}", [P, NT, H]) for s in "AB"}
        nm = {s: sb(f"nm_{s}", [P, NT, 2, 2, NPAIR], f32r) for s in "AB"}
        m_rows_t = sb("m_rows_t", [4 * H, L], f32r)
        m_t = {"A": m_rows_t[0:2 * H, :], "B": m_rows_t[2 * H:4 * H, :]}
        probs = sb("probs", [P, NSLOT, 2 * L])
        o_st = sb("o_st", [P, 2, 2 * L])
        rden = sb("rden", [P, NT, H])
        o_n = rot_s[:].rearrange("p (t d) -> p t d", t=NT)
        o_hi, o_lo = sb("o_hi", [P, NC, L], f32r), sb("o_lo", [P, NC, L], f32r)
        h_f = sb("h_f", [P, 2, 2 * L])
        h_hi, h_lo = sb("h_hi", [P, NF, L], f32r), sb("h_lo", [P, NF, L], f32r)

        def banks(name):
            t = es.enter_context(nc.psum_tensor(name, [P, 2 * 512], f32))
            return [t[:, 0:512], t[:, 512:1024]]

        gen_b, max_b, exp_b, pv_b = banks("gen"), banks("maxs"), banks("exps"), banks("pvs")

        gen_order = (["AlnT", "BctxT", "Ton0", "Ton1", "Aqk0", "ToT", "Aqk1", "Tout", "Av", "BlnT", "Bkv", "Bq", "ClnT"]
                     + [n for k in range(NF // 2) for n in (f"Ast{2 * k}", f"Cf{k}", f"Ast{2 * k + 1}")] + ["Cout"]
                     + [f"Bst{k}" for k in range(B_STACKS)] + ["AmT", "BmT", "Aon0", "Aon1", "AoT", "Aout"])
        gen_slot = {n: k % 2 for k, n in enumerate(gen_order)}

        def gen_bank(name):
            return gen_b[gen_slot[name]]

        def ring_bank(ring):
            return lambda name: ring[int(name[1:]) % 2]

        max_bank, exp_bank, pv_bank = ring_bank(max_b), ring_bank(exp_b), ring_bank(pv_b)

        ld_const, ld_w = sem("ld_const"), [sem("ld_w0"), sem("ld_w1")]
        w_hi_ready, w_lo_ready = sem("w_hi_ready"), sem("w_lo_ready")
        pool_zeroed, const_ready = sem("pool_zeroed"), sem("const_ready")
        gb_product, gb_ready = sem("gb_product"), sem("gb_ready")
        HELD = (w_hi_ready, 1)

        x_loaded, ctx_loaded, out_stored = (event(n, 1, 16) for n in ("x_loaded", "ctx_loaded", "out_stored"))
        xa_copied, xb_copied, xc_made = (event(n, 1) for n in ("xa_copied", "xb_copied", "xc_made"))

        def per_stage(what, stages, per, inc=1):
            return {s: event(f"{s}_{what}", per[s] if isinstance(per, dict) else per, inc) for s in stages}

        stat_done, mv_done, var_done = (per_stage(n, "ABC", k) for n, k in (("stat", NT), ("mv", NT), ("var", 1)))
        rstd_done, xn_done, ln_t = (per_stage(n, "ABC", k) for n, k in (("rstd", 1), ("xn", NT), ("lnT", 1)))
        t_done, thi_done, tlo_done = (per_stage(n, "ABC", k) for n, k in (("t", NC), ("thi", 1), ("tlo", 1)))
        ctx_t, ctx_hi, ctx_lo = event("ctx_t", 1), event("ctx_hi", 1), event("ctx_lo", 1)
        a_proj, b_kv, b_q = event("a_proj", NT + 1), event("b_kv", 1), event("b_q", 1)
        v_ready = per_stage("v", "AB", 1)
        TILES = {"A": NT, "B": NT + 1}
        cos_done, sin_done = (per_stage(n, "AB", TILES) for n in ("cos", "sin"))
        rot_done = per_stage("rot", "AB", {s: 2 * n for s, n in TILES.items()})
        PIECES = {"A": 2 * NT, "B": NT + 1}
        nhi_done = per_stage("nhi", "AB", PIECES)
        nlo_done = per_stage("nlo", "AB", PIECES)
        STACKS, MAXES, EXPS = ({"A": a, "B": b} for a, b in ((A_STACKS, B_STACKS), (A_MAX, B_MAX), (A_EXP, B_EXP)))
        st_t, st_done = per_stage("stT", "AB", STACKS), per_stage("st", "AB", {"A": A_STACKS, "B": B_STACKS + 2})
        score, mx_done = per_stage("score", "AB", MAXES), per_stage("mx", "AB", MAXES)
        nmhi_done, nm_done = per_stage("nmhi", "AB", NT), per_stage("nm", "AB", NT)
        m_tr, m_copied, m_rows = (per_stage(n, "AB", 1) for n in ("mT", "mcopy", "mrows"))
        m_rows = {s: Event(e.sem, 4, 16, HELD) for s, e in m_rows.items()}
        shifted, p_done = per_stage("shifted", "AB", EXPS), per_stage("p", "AB", EXPS)
        pv, o_copied = per_stage("pv", "AB", NG), per_stage("ocopy", "AB", 2)
        o_nat, rden_done, on_done = (per_stage(n, "AB", NT) for n in ("onat", "rden", "on"))
        o_tr, ohi_done, olo_done = (per_stage(n, "AB", 1) for n in ("oT", "ohi", "olo"))
        proj_out = per_stage("proj", "ABC", 1)
        res_done = per_stage("res", "ABC", 1)
        f1, gelu_done = event("f1", NF // 2), event("gelu", NF)
        hhi_done, hlo_done = event("hhi", NF // 2), event("hlo", NF // 2)

        block = es.enter_context(nc.Block())

        @block.sync
        def _(sp):
            def const(dst, src):
                sp.dma_start(dst, src).then_inc(ld_const, 16)

            const(cond_s[:], cond_t.rearrange("(c p) b -> p c b", p=P))
            for k, t in enumerate((rot_c, o_st, h_f)):
                const(t[:].rearrange("p a b -> p (a b)").rearrange("p (c n) -> p c n", c=NC),
                      lnw[k].rearrange("(c p) n -> p c n", p=P))
            const(lnb_t[:], lnb)
            const(rope_t[:].rearrange("p t k d -> p t (k d)"), rope.rearrange("(t p) n -> p t n", p=P))
            const(b1_t[:], b1)
            const(b2_t[:], b2[None, :].to_broadcast([P, D]))
            sp.dma_start(x_in[:], x_d[0]).then_inc(x_loaded.sem, 16)
            for k, (n, cols, src) in enumerate(names):
                if k >= 2:
                    sp.wait_ge(w_lo_ready, k - 1)
                stage = probs[:, 4 * (k % 2):4 * (k % 2) + 4, :].rearrange("p a b -> p (a b)")[:, 0:cols]
                sp.dma_start(stage.rearrange("p (c n) -> p c n", c=src.shape[0] // P),
                             src.rearrange("(c p) n -> p c n", p=P)).then_inc(ld_w[k % 2], 16)

            def body(turn, has):
                if "N" in has and "A" in has:
                    sp.wait_ge(*xa_copied.at(turn))
                    sp.wait_ge(*xn_done["A"].at(turn))
                    sp.dma_start(x_in[:], x_d[turn.times(1, 1)]).then_inc(x_loaded.sem, 16)
                if "A" in has:
                    sp.wait_ge(*ctx_t.at(turn + -1))
                    sp.dma_start(ctx_in[:], ctx[turn.times(1)]).then_inc(ctx_loaded.sem, 16)
                if "C" in has:
                    sp.wait_ge(*res_done["C"].at(turn + -2))
                    sp.dma_start(out_d[turn.times(1, -2)], xc[:]).then_inc(out_stored.sem, 16)
                for s in "AB":
                    if s in has:
                        sp.wait_ge(*m_copied[s].at(turn + STAGE[s]))
                        for par in range(2):
                            for j in range(2):
                                row, r0 = SROW * par + NS + j, (par * 2 + j) * NPAIR
                                sp.dma_start(q_st[s][row:row + 1, :, :].bitcast(f32),
                                             m_t[s][r0:r0 + NPAIR, :].bitcast(f32)).then_inc(m_rows[s].sem, 16)
            run_turns(sp, [], body)
            sp.wait_ge(out_stored.sem, 16 * B)

        @block.gpsimd
        def _(pool):
            g = nc.gpsimd
            v_a_ht = v_a[:].rearrange("p t h w -> p (t h) w")
            k_nat_ht = k_nat[:].rearrange("p t h w -> p (t h) w")
            g.memset(ident[:], 0.0).then_inc(pool_zeroed, 1)
            g.memset(minus_half[:], -0.5).then_inc(const_ready, 1)
            g.memset(v_a_ht[:, :, DH:VW], 0.0).then_inc(pool_zeroed, 1)
            g.memset(v_b[:, :, DH:VW], 0.0).then_inc(pool_zeroed, 1)
            g.memset(q_nat[:].bitcast(f32), 0.0).then_inc(pool_zeroed, 1)
            g.memset(k_nat[:].bitcast(f32), 0.0).then_inc(pool_zeroed, 1)
            g.memset(k_st_b[:].bitcast(f32), 0.0).then_inc(pool_zeroed, 1)
            pool.wait_ge(pool_zeroed, 6)
            g.affine_select(out=ident[:], in_=ident[:], compare_op=ALU.not_equal, fill=1.0, base=0,
                            pattern=[[-1, P]], channel_multiplier=1).then_inc(pool_zeroed, 1)
            g.memset(v_a_ht[:, :, DH:DH + 1], 1.0).then_inc(const_ready, 1)
            g.memset(v_b[:, :, DH:DH + 1], 1.0).then_inc(const_ready, 1)
            g.memset(k_nat_ht[:, :, NS:NSM].bitcast(f32), 1.0).then_inc(const_ready, 1)
            pool.wait_ge(pool_zeroed, 7)
            g.tensor_copy(ident_r[:], ident[:]).then_inc(const_ready, 1)
            for k, (n, cols, _) in enumerate(names):
                a = w_at[n][0]
                pool.wait_ge(w_hi_ready, k + 1)
                stage = probs[:, 4 * (k % 2):4 * (k % 2) + 4, :].rearrange("p a b -> p (a b)")[:, 0:cols]
                g.tensor_tensor(w_lo[:, a:a + cols], stage, w_hi[:, a:a + cols].bitcast(f32), ALU.subtract)\
                    .then_inc(w_lo_ready, 1)

            def copy(out_, in_, column):
                g.tensor_tensor(pool_fence[:, column:column + 1], minus_half[:, 0:1], minus_half[:, 0:1], ALU.mult)
                return g.tensor_copy(out_, in_)

            def power(s, bt):
                pool.wait_ge(*var_done[s].at(bt))
                pool.wait_ge(*xn_done[s].at(bt + -1))
                g.tensor_tensor(rstd[s][:], ve[s][:], minus_half[:], ALU.pow).then_inc(rstd_done[s].sem, 1)

            def body(turn, has):
                A, Bb, C = turn, turn + -1, turn + -2
                if "C" in has:
                    power("C", C)
                    pool.wait_ge(*xn_done["C"].at(C))
                    pool.wait_ge(*out_stored.at(C + -1))
                    g.tensor_tensor(xc[:], xb[:], b2_t[:, None, :].to_broadcast([P, NT, D]), ALU.add)\
                        .then_inc(xc_made.sem, 1)
                if "B" in has:
                    pool.wait_ge(*xn_done["B"].at(Bb))
                    pool.wait_ge(*xc_made.at(Bb + -1))
                    copy(xb[:], xa[:], 0).then_inc(xb_copied.sem, 1)
                if "A" in has:
                    pool.wait_ge(*x_loaded.at(A))
                    pool.wait_ge(*xb_copied.at(A + -1))
                    copy(xa[:], x_in[:], 1).then_inc(xa_copied.sem, 1)
                if "C" in has:
                    for k in range(NF // 2):
                        pool.wait_ge(*hhi_done.at(C, k + 1))
                        if k == 0:
                            pool.wait_ge(*proj_out["C"].at(C + -1))
                        g.tensor_tensor(h_lo[:, 2 * k:2 * k + 2, :],
                                        h_f[:, k % 2, :].rearrange("p (c n) -> p c n", c=2),
                                        h_hi[:, 2 * k:2 * k + 2, :].bitcast(f32), ALU.subtract)\
                            .then_inc(hlo_done.sem, 1)
                if "N" in has:
                    power("A", turn + 1)
                if "A" in has:
                    power("B", A)
            run_turns(pool, [], body)

        @block.scalar
        def _(act):
            s_ = nc.scalar
            t_use = Reuse(HELD, [(s, 0, tlo_done[s], 1) for s in "ABC"])
            p_use = Reuse(HELD, [(f"A{h}", h % NSLOT, pv["A"], h // GRP + 1) for h in range(A_EXP)]
                          + [(f"B{k}", k, pv["B"], k // 2 + 1) for k in range(B_EXP)])
            o_use = Reuse(HELD, [(f"{s}{k}", k, o_nat[s], NT) for s in "AB" for k in range(2)])
            oh_use = Reuse(HELD, [("T", 0, proj_out["B"], 1), ("A", 0, proj_out["A"], 1)])
            nat_use = Reuse(HELD, [("A", 0, st_t["A"], A_STACKS), ("B", 0, st_t["B"], B_STACKS)])
            h_use = Reuse(HELD, [(f"C{k}", k % 2, hlo_done, k + 1) for k in range(NF // 2)])

            def column(ln, c, bt):
                return gb[:, ln, c, bt.off:bt.off + 1] if bt.reg is None else gb[:, ln, c, bass.ds(bt.times(1), 1)]

            def modulate(s, turn):
                bt, ln = turn + STAGE[s], "ABC".index(s)
                act.wait_ge(*ln_t[s].at(bt))
                act.wait_ge(*t_use.before(s, turn))
                for c in range(NC):
                    s_.activation(t_f[:, c, :], gen_bank(s + "lnT")[:, c * L:(c + 1) * L], ACT.Identity,
                                  scale=column(ln, c, bt), bias=column(ln, NC + c, bt)).then_inc(t_done[s].sem, 1)

            def stack_high(s, bt, k, rot_k, src, dst, blocks):
                act.wait_ge(*rot_done[s].at(bt, 2 * rot_k + 2))
                out_ = dst[:, :, 0:NS].rearrange("p h (b d) -> p h b d", d=DH)[:, :, blocks, :]
                s_.activation(out_, src.rearrange("p (h d) -> p h d", d=DH)[:, :, None, :]
                              .to_broadcast([out_.shape[0], H, 2, DH]), ACT.Copy).then_inc(nhi_done[s].sem, 1)

            def stack_a(bt, k):
                act.wait_ge(*st_t["A"].at(bt, k + 1))
                if k == 0:
                    act.wait_ge(*shifted["A"].at(bt + -1))
                dst = q_st["A"] if k < A_STACKS // 2 else k_st_a
                p0 = 2 * (k % (A_STACKS // 2))
                s_.activation(dst[:, p0:p0 + 2, :], gen_bank(f"Ast{k}").rearrange("p (a n) -> p a n", a=2),
                              ACT.Copy).then_inc(st_done["A"].sem, 1)

            def stacks_b(bt):
                for k in range(B_STACKS):
                    act.wait_ge(*st_t["B"].at(bt, k + 1))
                    if k == 0:
                        act.wait_ge(*shifted["B"].at(bt + -1))
                    src = gen_bank(f"Bst{k}")
                    if k < NPAIR // 2:
                        s_.activation(q_st["B"][:, 2 * k:2 * k + 2, :], src.rearrange("p (a n) -> p a n", a=2),
                                      ACT.Copy).then_inc(st_done["B"].sem, 1)
                    else:
                        p0 = 4 * (k - NPAIR // 2)
                        for par in range(2):
                            r = slice(SROW * par, SROW * (par + 1))
                            s_.activation(k_st_b[r, p0:p0 + 4, par, 0:LC],
                                          src[r, :].rearrange("p (a n) -> p a n", a=4)[:, :, 0:LC],
                                          ACT.Copy).then_inc(st_done["B"].sem, 1)

            def max_rows(s, bt):
                act.wait_ge(*m_tr[s].at(bt))
                act.wait_ge(*m_rows[s].at(bt + -1))
                s_.activation(m_t[s], gen_bank(s + "mT")[0:2 * H, 0:L], ACT.Copy).then_inc(m_copied[s].sem, 1)

            def exps(s, turn, k, rows):
                act.wait_ge(*shifted[s].at(turn + STAGE[s], k + 1))
                act.wait_ge(*p_use.before(f"{s}{k}", turn))
                s_.activation(probs[0:rows, k % NSLOT, :], exp_bank(f"{s}{k}")[0:rows, :], ACT.Exp,
                              scale=SCALE).then_inc(p_done[s].sem, 1)

            def outputs(s, turn, k):
                act.wait_ge(*pv[s].at(turn + STAGE[s], 2 * k + 2))
                act.wait_ge(*o_use.before(f"{s}{k}", turn))
                s_.activation(o_st[:, k, :], pv_bank(f"{s}{k}"), ACT.Copy).then_inc(o_copied[s].sem, 1)

            def output_high(t_, s, turn):
                act.wait_ge(*o_tr[s].at(turn + STAGE[t_]))
                act.wait_ge(*oh_use.before(t_, turn))
                s_.activation(o_hi[:].rearrange("p c n -> p (c n)"), gen_bank(t_ + "oT"), ACT.Copy)\
                    .then_inc(ohi_done[s].sem, 1)

            act.wait_ge(gb_ready, 12)
            act.wait_ge(const_ready, 5)
            act.wait_ge(w_lo_ready, len(names))

            def body(turn, has):
                A, Bb, C = turn, turn + -1, turn + -2
                if "A" in has:
                    modulate("A", turn)
                if "B" in has:
                    act.wait_ge(*ctx_t.at(Bb))
                    act.wait_ge(*b_kv.at(Bb + -1))
                    s_.activation(c_hi[:].rearrange("p c n -> p (c n)"), gen_bank("BctxT")[:, 0:NC * LC], ACT.Copy)\
                        .then_inc(ctx_hi.sem, 1)
                if "T" in has:
                    output_high("T", "B", turn)
                if "A" in has:
                    act.wait_ge(*nat_use.before("A", turn))
                    for t in range(NT):
                        stack_high("A", A, 2 * t, t, rot_c[:, t, 0:D], q_nat[:, t], slice(0, 3, 2))
                        stack_high("A", A, 2 * t + 1, t, rot_c[:, t, D:2 * D], k_nat[:, t], slice(0, 2))
                    act.wait_ge(*a_proj.at(A, NT + 1))
                    act.wait_ge(*pv["A"].at(A + -1))
                    s_.activation(v_a[:].rearrange("p t h w -> p (t h) w")[:, :, 0:DH],
                                  gen_bank("Av").rearrange("p (a d) -> p a d", d=DH), ACT.Copy)\
                        .then_inc(v_ready["A"].sem, 1)
                if "B" in has:
                    modulate("B", turn)
                    act.wait_ge(*b_kv.at(Bb))
                    act.wait_ge(*pv["B"].at(Bb + -1))
                    s_.activation(v_b[:, :, 0:DH],
                                  gen_bank("Bkv")[0:LC, D:2 * D].rearrange("p (h d) -> p h d", d=DH), ACT.Copy)\
                        .then_inc(v_ready["B"].sem, 1)
                if "C" in has:
                    modulate("C", turn)
                for k in range(NF // 2):
                    if "A" in has:
                        stack_a(A, 2 * k)
                    if "C" in has:
                        act.wait_ge(*f1.at(C, k + 1))
                        act.wait_ge(*h_use.before(f"C{k}", turn))
                        for j in range(2):
                            s_.activation(h_f[:, k % 2, j * L:(j + 1) * L], gen_bank(f"Cf{k}")[:, j * L:(j + 1) * L],
                                          ACT.Gelu, bias=b1_t[:, 2 * k + j:2 * k + j + 1]).then_inc(gelu_done.sem, 1)
                    if "A" in has:
                        stack_a(A, 2 * k + 1)
                if "B" in has:
                    act.wait_ge(*nat_use.before("B", turn))
                    stack_high("B", Bb, 0, 0, rk_c[:, :], k_nat[0:LC, 0], slice(0, 2))
                    for t in range(NT):
                        stack_high("B", Bb, t + 1, t + 1, rot_c[:, t, 0:D], q_nat[:, t], slice(0, 3, 2))
                    stacks_b(Bb)
                if "A" in has:
                    max_rows("A", A)
                    for h in range(A_EXP):
                        exps("A", turn, h, P)
                        if h == 3 and "B" in has:
                            max_rows("B", Bb)
                        if h == 11:
                            outputs("A", turn, 0)
                    outputs("A", turn, 1)
                elif "B" in has:
                    max_rows("B", Bb)
                if "B" in has:
                    for k in range(4):
                        exps("B", turn, k, LC)
                if "A" in has:
                    output_high("A", "A", turn)
                if "B" in has:
                    for k in range(4, B_EXP):
                        exps("B", turn, k, LC)
                    outputs("B", turn, 0)
                    outputs("B", turn, 1)
            run_turns(act, [t_use, p_use, o_use, oh_use, h_use, nat_use], body)

        @block.vector
        def _(dve):
            v = nc.vector
            for k, (n, cols, _) in enumerate(names):
                a = w_at[n][0]
                dve.wait_ge(ld_w[k % 2], 16 * (k // 2 + 1))
                stage = probs[:, 4 * (k % 2):4 * (k % 2) + 4, :].rearrange("p a b -> p (a b)")[:, 0:cols]
                v.tensor_copy(w_hi[:, a:a + cols], stage).then_inc(w_hi_ready, 1)
                if k == 0:
                    dve.wait_ge(gb_product, 1)
                    for m in range(12):
                        v.tensor_scalar(gb[:, m // 4, m % 4, :], gen_b[0][:, m * B:(m + 1) * B], lnb_t[:, m:m + 1],
                                        1.0 if m % 4 < NC else 0.0, ALU.add, ALU.add).then_inc(gb_ready, 1)
            dve.wait_ge(gb_ready, 12)

            rot_use = Reuse(HELD, [("A0", 0, nlo_done["A"], 2), ("A1", 1, nlo_done["A"], 4),
                                   ("B0", 0, nlo_done["B"], 2), ("B1", 1, nlo_done["B"], 3)])
            rots_use = Reuse(HELD, [("To", 0, o_tr["B"], 1), ("A0", 0, rot_done["A"], 2), ("A1", 0, rot_done["A"], 4),
                                    ("B0", 0, rot_done["B"], 4), ("B1", 0, rot_done["B"], 6),
                                    ("Ao", 0, o_tr["A"], 1)])
            ol_use = Reuse(HELD, [("T", 0, proj_out["B"], 1), ("A", 0, proj_out["A"], 1)])
            nat_use = Reuse(HELD, [("A", 0, st_t["A"], A_STACKS), ("B", 0, st_t["B"], B_STACKS)])
            norm_used = {"A": a_proj, "B": b_q, "C": f1}

            def split_norm(s, bt):
                dve.wait_ge(*t_done[s].at(bt))
                dve.wait_ge(*norm_used[s].at(bt + -1))
                v.tensor_copy(t_hi[s][:], t_f[:]).then_inc(thi_done[s].sem, 1)
                dve.wait_ge(*thi_done[s].at(bt))
                v.tensor_tensor(t_lo[s][:], t_f[:], t_hi[s][:].bitcast(f32), ALU.subtract)\
                    .then_inc(tlo_done[s].sem, 1)

            def stack_low(s, bt, k, src, dst, block):
                dve.wait_ge(*nhi_done[s].at(bt, k + 1))
                v.tensor_tensor(dst[:, :, block * DH:(block + 1) * DH], src.rearrange("p (h d) -> p h d", d=DH),
                                dst[:, :, 0:DH].bitcast(f32), ALU.subtract).then_inc(nlo_done[s].sem, 1)

            def rotation(s, bt, k, src, cos_out, sin_out, t, rows):
                n = src.shape[-1] // DH
                cosv = rope_t[0:rows, t, None, 0:1, :].to_broadcast([rows, n, 2, 8])
                sinv = rope_t[0:rows, t, None, 1:3, :].to_broadcast([rows, n, 2, 8])
                sv = src.rearrange("p (h s d) -> p h s d", s=2, d=8)
                cv = cos_out.rearrange("p (h s d) -> p h s d", s=2, d=8)
                ov = sin_out.rearrange("p (h s d) -> p h s d", s=2, d=8)
                v.tensor_tensor(cv, sv, cosv, ALU.mult).then_inc(cos_done[s].sem, 1)
                v.tensor_tensor(ov, sv, sinv, ALU.mult).then_inc(sin_done[s].sem, 1)
                dve.wait_ge(*sin_done[s].at(bt, k + 1))
                for half in range(2):
                    v.tensor_tensor(cv[:, :, half, :], cv[:, :, half, :], ov[:, :, 1 - half, :], ALU.add)\
                        .then_inc(rot_done[s].sem, 1)

            def norm_statistics(s, bt, src):
                for t in range(NT):
                    v.bn_stats(stats[s][:, t, :], src[:, t, :]).then_inc(stat_done[s].sem, 1)
                dve.wait_ge(*stat_done[s].at(bt))
                v.memset(fence[s][:], 0.0)
                for t in range(NT):
                    v.bn_aggr(mv[s][:, t, :], stats[s][:, t, :]).then_inc(mv_done[s].sem, 1)
                dve.wait_ge(*mv_done[s].at(bt))
                dve.wait_ge(*rstd_done[s].at(bt + -1))
                v.tensor_scalar(ve[s][:], mv[s][:, :, 1], EPS, None, ALU.add).then_inc(var_done[s].sem, 1)

            def normalise(s, bt, src):
                dve.wait_ge(*rstd_done[s].at(bt))
                dve.wait_ge(*ln_t[s].at(bt + -1))
                for t in range(NT):
                    v.tensor_scalar(xn[s][:, t, :], src[:, t, :], mv[s][:, t, 0:1], rstd[s][:, t:t + 1],
                                    ALU.subtract, ALU.mult).then_inc(xn_done[s].sem, 1)

            def maxima(s, bt, k, out_, src):
                dve.wait_ge(*score[s].at(bt, k + 1))
                if k == 0:
                    dve.wait_ge(*nm_done[s].at(bt + -1))
                v.reduce_max(out_, src, AX.X).then_inc(mx_done[s].sem, 1)

            def negate(s, bt, t):
                dve.wait_ge(*mx_done[s].at(bt, (t + 1) * MAXES[s] // NT))
                if t == 0:
                    dve.wait_ge(*m_tr[s].at(bt + -1))
                mv_ = mx[s][:, t, :].rearrange("p (a q) -> p q a", q=2)
                v.tensor_scalar(nm[s][:, t, :, 0, :], mv_, -1.0, None, ALU.mult).then_inc(nmhi_done[s].sem, 1)
                dve.wait_ge(*nmhi_done[s].at(bt, t + 1))
                v.scalar_tensor_tensor(out=nm[s][:, t, :, 1, :], in0=mv_, scalar=-1.0,
                                       in1=nm[s][:, t, :, 0, :].bitcast(f32), op0=ALU.mult,
                                       op1=ALU.subtract).then_inc(nm_done[s].sem, 1)

            def divide(t_, s, turn):
                bt = turn + STAGE[t_]
                for t in range(NT):
                    dve.wait_ge(*o_nat[s].at(bt, t + 1))
                    src = gen_bank(f"{t_}on{t}").rearrange("p (h w) -> p h w", w=VW)
                    if t == 0:
                        dve.wait_ge(*rots_use.before(t_ + "o", turn))
                    v.reciprocal(rden[:, t, :], src[:, :, DH]).then_inc(rden_done[s].sem, 1)
                    dve.wait_ge(*rden_done[s].at(bt, t + 1))
                    v.tensor_tensor(o_n[:, t, :].rearrange("p (h d) -> p h d", d=DH), src[:, :, 0:DH],
                                    rden[:, t, :, None].to_broadcast([P, H, DH]), ALU.mult)\
                        .then_inc(on_done[s].sem, 1)

            def output_low(t_, s, turn):
                dve.wait_ge(*ohi_done[s].at(turn + STAGE[t_]))
                dve.wait_ge(*ol_use.before(t_, turn))
                v.tensor_tensor(o_lo[:].rearrange("p c n -> p (c n)"), gen_bank(t_ + "oT"),
                                o_hi[:].rearrange("p c n -> p (c n)").bitcast(f32), ALU.subtract)\
                    .then_inc(olo_done[s].sem, 1)

            def residual(s, bt, bank, acc, moved):
                dve.wait_ge(*proj_out[s].at(bt))
                dve.wait_ge(*moved.at(bt))
                flat = acc[:].rearrange("p t d -> p (t d)")
                v.tensor_tensor(flat, bank, flat, ALU.add).then_inc(res_done[s].sem, 1)
                dve.wait_ge(*res_done[s].at(bt))

            def body(turn, has):
                A, Bb, C = turn, turn + -1, turn + -2

                def rotation_a(t):
                    dve.wait_ge(*a_proj.at(A, t + 1))
                    dve.wait_ge(*rot_use.before(f"A{t}", turn))
                    dve.wait_ge(*rots_use.before(f"A{t}", turn))
                    rotation("A", A, t, gen_bank(f"Aqk{t}"), rot_c[:, t, :], rot_s[:, :], t, P)

                if "A" in has:
                    split_norm("A", A)
                if "B" in has:
                    dve.wait_ge(*ctx_hi.at(Bb))
                    dve.wait_ge(*b_kv.at(Bb + -1))
                    v.tensor_tensor(c_lo[:].rearrange("p c n -> p (c n)"), gen_bank("BctxT")[:, 0:NC * LC],
                                    c_hi[:].rearrange("p c n -> p (c n)").bitcast(f32), ALU.subtract)\
                        .then_inc(ctx_lo.sem, 1)
                if "T" in has:
                    divide("T", "B", turn)
                if "B" in has:
                    normalise("B", Bb, xa)
                if "A" in has:
                    rotation_a(0)
                if "T" in has:
                    output_low("T", "B", turn)
                if "A" in has:
                    rotation_a(1)
                if "T" in has:
                    residual("B", C, gen_bank("Tout"), xb, xb_copied)
                    norm_statistics("C", C, xb)
                if "A" in has:
                    for t in range(NT):
                        if t == 0:
                            dve.wait_ge(*nat_use.before("A", turn))
                        stack_low("A", A, 2 * t, rot_c[:, t, 0:D], q_nat[:, t], 1)
                        stack_low("A", A, 2 * t + 1, rot_c[:, t, D:2 * D], k_nat[:, t], 2)
                if "T" in has:
                    normalise("C", C, xb)
                if "B" in has:
                    split_norm("B", Bb)
                    dve.wait_ge(*v_ready["B"].at(Bb))
                    rotation("B", Bb, 0, gen_bank("Bkv")[0:LC, 0:D], rk_c[:, :], rk_s[:, :], 0, LC)
                    dve.wait_ge(*b_q.at(Bb))
                    for t in range(NT):
                        dve.wait_ge(*rot_use.before(f"B{t}", turn))
                        dve.wait_ge(*rots_use.before(f"B{t}", turn))
                        rotation("B", Bb, t + 1, gen_bank("Bq")[:, t * D:(t + 1) * D], rot_c[:, t, 0:D],
                                 rot_s[:, 0:D], t, P)
                if "C" in has:
                    split_norm("C", C)
                    for k in range(NF // 2):
                        dve.wait_ge(*gelu_done.at(C, 2 * k + 2))
                        if k == 0:
                            dve.wait_ge(*proj_out["C"].at(C + -1))
                        v.tensor_copy(h_hi[:, 2 * k:2 * k + 2, :],
                                      h_f[:, k % 2, :].rearrange("p (c n) -> p c n", c=2)).then_inc(hhi_done.sem, 1)
                if "B" in has:
                    dve.wait_ge(*nat_use.before("B", turn))
                    stack_low("B", Bb, 0, rk_c[:, :], k_nat[0:LC, 0], 2)
                    for t in range(NT):
                        stack_low("B", Bb, t + 1, rot_c[:, t, 0:D], q_nat[:, t], 1)
                if "A" in has:
                    for k in range(A_MAX):
                        t, pair, par = k // NPAIR, 2 * (k % NPAIR // 2), k % 2
                        maxima("A", A, k, mx["A"][:, t, :].rearrange("p (a q) -> p q a", q=2)[:, par, pair:pair + 2],
                               max_bank(f"A{k}").rearrange("p (a n) -> p a n", a=2))
                        if k % NPAIR == NPAIR - 1:
                            negate("A", A, t)
                if "C" in has:
                    residual("C", C, gen_bank("Cout"), xc, xc_made)
                if "B" in has:
                    for k in range(B_MAX):
                        t, c = k // (NPAIR // 2), k % (NPAIR // 2)
                        maxima("B", Bb, k, mx["B"][:, t, 4 * c:4 * c + 4],
                               max_bank(f"B{k}").rearrange("p (a n) -> p a n", a=4)[:, :, 0:LC])
                        if c == NPAIR // 2 - 1:
                            negate("B", Bb, t)
                if "N" in has:
                    dve.wait_ge(*x_loaded.at(turn + 1))
                    norm_statistics("A", turn + 1, x_in)
                    normalise("A", turn + 1, x_in)
                if "A" in has:
                    divide("A", "A", turn)
                    output_low("A", "A", turn)
                    residual("A", A, gen_bank("Aout"), xa, xa_copied)
                    norm_statistics("B", A, xa)
            run_turns(dve, [rot_use, rots_use, ol_use, nat_use], body)

        @block.tensor
        def _(pe):
            mm, tr = nc.tensor.matmul, nc.tensor.transpose
            wqkv_, wsa_, wq_, wkv_, wca_, w1_ = (weight(n, NC) for n in ("qkv", "sa", "q", "kv", "ca", "w1"))
            w2_ = weight("w2", NF)

            rel = {"AlnT": (t_done["A"], NC), "ClnT": (t_done["C"], NC), "BlnT": (t_done["B"], NC),
                   "BctxT": (ctx_lo, 1), "Av": (v_ready["A"], 1), "Bkv": (sin_done["B"], 1),
                   "Bq": (sin_done["B"], NT + 1)}
            for t in range(NT):
                rel[f"Aqk{t}"] = (sin_done["A"], t + 1)
            for k in range(NF // 2):
                rel[f"Cf{k}"] = (gelu_done, 2 * k + 2)
            for k in range(A_STACKS):
                rel[f"Ast{k}"] = (st_done["A"], k + 1)
            for k in range(B_STACKS):
                rel[f"Bst{k}"] = (st_done["B"], k + 1 if k < NPAIR // 2 else 2 * (k + 1) - NPAIR // 2)
            for t_, s in (("A", "A"), ("T", "B")):
                rel[s + "mT"], rel[t_ + "oT"], rel[t_ + "out"] = (m_copied[s], 1), (olo_done[s], 1), (res_done[s], 1)
                for t in range(NT):
                    rel[f"{t_}on{t}"] = (on_done[s], t + 1)
            rel["Cout"] = (res_done["C"], 1)
            gen_use = Reuse(HELD, [(n, gen_slot[n], *rel[n]) for n in gen_order])
            max_use = Reuse(HELD, [(f"{s}{k}", k % 2, mx_done[s], k + 1) for s in "AB" for k in range(MAXES[s])])
            exp_use = Reuse(HELD, [(f"{s}{k}", k % 2, p_done[s], k + 1) for s in "AB" for k in range(EXPS[s])])
            pv_use = Reuse(HELD, [(f"{s}{k}", k, o_copied[s], k + 1) for s in "AB" for k in range(2)])

            def gen(name, turn):
                pe.wait_ge(*gen_use.before(name, turn))
                return gen_bank(name)

            def split_product(out_, terms):
                n = len(terms)
                for k, (l, r) in enumerate(terms):
                    last = mm(out_, l, r, start=(k == 0), stop=(k == n - 1))
                return last

            def norm_transpose(s, turn):
                pe.wait_ge(*xn_done[s].at(turn + STAGE[s]))
                o = gen(s + "lnT", turn)
                for c in range(NC):
                    for t in range(NT):
                        last = tr(o[:, c * L + t * P:c * L + (t + 1) * P], xn[s][:, t, c * P:(c + 1) * P], ident[:])
                last.then_inc(ln_t[s].sem, 1)

            def three(xh, xl, w, xs, ws, chunks):
                wh, wl = w
                return [(x_[:, c, xs], w_[:, c, ws]) for c in range(chunks)
                        for x_, w_ in ((xh, wh), (xl, wh), (xh, wl))]

            def stack_transposes(s, turn, k, jobs):
                o = gen(f"{s}st{k}", turn)
                for col, src, rows in jobs:
                    last = tr(o[:, col:col + rows].bitcast(f32r), src, ident_r[0:rows, 0:rows])
                last.then_inc(st_t[s].sem, 1)

            def pair_of(nat_, t, p, rows=P):
                return nat_[0:rows, t, 2 * p:2 * p + 2, :].rearrange("p h w -> p (h w)")

            def max_transpose(s, turn):
                pe.wait_ge(*nm_done[s].at(turn + STAGE[s]))
                o = gen(s + "mT", turn)
                for t in range(NT):
                    last = tr(o[0:2 * H, t * P:(t + 1) * P].bitcast(f32r),
                              nm[s][:, t].rearrange("p q j a -> p (q j a)"), ident_r[:])
                last.then_inc(m_tr[s].sem, 1)

            def scores_a(turn, k):
                t, pair, par = k // NPAIR, 2 * (k % NPAIR // 2), k % 2
                pe.wait_ge(*max_use.before(f"A{k}", turn))
                o = max_bank(f"A{k}")
                r = slice(SROW * par, SROW * par + NS)
                for j in range(2):
                    last = mm(o[:, j * L:(j + 1) * L], q_st["A"][r, pair + j, t * P:(t + 1) * P],
                              k_st_a[r, pair + j, :], start=True, stop=True)
                last.then_inc(score["A"].sem, 1)

            def scores_b(turn, k):
                t, c = k // (NPAIR // 2), k % (NPAIR // 2)
                pe.wait_ge(*max_use.before(f"B{k}", turn))
                o = max_bank(f"B{k}")
                for j in range(2):
                    last = mm(o[:, j * L:(j + 1) * L], q_st["B"][:, 2 * c + j, t * P:(t + 1) * P],
                              k_st_b[:, 2 * c + j].rearrange("p q n -> p (q n)"), start=True, stop=True)
                last.then_inc(score["B"].sem, 1)

            def shifted_a(turn, h):
                pe.wait_ge(*exp_use.before(f"A{h}", turn))
                o, pair = exp_bank(f"A{h}"), h // 2
                r = slice(SROW * (h % 2), SROW * (h % 2) + NSM)
                for t in range(NT):
                    last = mm(o[:, t * L:(t + 1) * L], k_st_a[r, pair, t * P:(t + 1) * P], q_st["A"][r, pair, :],
                              start=True, stop=True)
                last.then_inc(shifted["A"].sem, 1)

            def shifted_b(turn, pair):
                pe.wait_ge(*exp_use.before(f"B{pair}", turn))
                o = exp_bank(f"B{pair}")
                for par in range(2):
                    last = mm(o[0:LC, par * L:(par + 1) * L], k_st_b[:, pair, par, 0:LC], q_st["B"][:, pair, :],
                              start=True, stop=True)
                last.then_inc(shifted["B"].sem, 1)

            def weighted(s, turn, g_):
                bt = turn + STAGE[s]
                pe.wait_ge(*p_done[s].at(bt, (g_ + 1) * EXPS[s] // NG))
                if g_ == 0:
                    pe.wait_ge(*v_ready[s].at(bt))
                if g_ % 2 == 0:
                    pe.wait_ge(*pv_use.before(f"{s}{g_ // 2}", turn))
                o = pv_bank(f"{s}{g_ // 2}")[:, (g_ % 2) * L:(g_ % 2 + 1) * L]
                for t in range(NT if s == "A" else 1):
                    for j in range(GRP):
                        h = GRP * g_ + j
                        if s == "A":
                            l, r = v_a[:, t, h, :], probs[:, h % NSLOT, t * L:(t + 1) * L]
                        else:
                            l, r = v_b[:, h, :], probs[0:LC, h // 2, (h % 2) * L:(h % 2 + 1) * L]
                        last = mm(o[VW * j:VW * (j + 1), :], l, r, start=(t == 0),
                                  stop=(s == "B" or t == NT - 1))
                last.then_inc(pv[s].sem, 1)

            def output_natural(t_, s, turn):
                for t in range(NT):
                    if t == 0:
                        pe.wait_ge(*o_copied[s].at(turn + STAGE[t_]))
                    o = gen(f"{t_}on{t}", turn)
                    for g_ in range(NG):
                        last = tr(o[:, g_ * P:(g_ + 1) * P],
                                  o_st[:, g_ // 2, (g_ % 2) * L + t * P:(g_ % 2) * L + (t + 1) * P], ident[:])
                    last.then_inc(o_nat[s].sem, 1)

            def output_transpose(t_, s, turn):
                pe.wait_ge(*on_done[s].at(turn + STAGE[t_]))
                o = gen(t_ + "oT", turn)
                for c in range(NC):
                    for t in range(NT):
                        last = tr(o[:, c * L + t * P:c * L + (t + 1) * P], o_n[:, t, c * P:(c + 1) * P], ident[:])
                last.then_inc(o_tr[s].sem, 1)

            def output_product(t_, s, turn):
                pe.wait_ge(*olo_done[s].at(turn + STAGE[t_]))
                o = gen(t_ + "out", turn)
                for t in range(NT):
                    last = split_product(o[:, t * D:(t + 1) * D],
                                         three(o_hi, o_lo, wsa_ if s == "A" else wca_, slice(t * P, (t + 1) * P),
                                               slice(0, D), NC))
                last.then_inc(proj_out[s].sem, 1)

            pe.wait_ge(ld_const, 8 * 16)
            for m in range(12):
                w = (rot_c, o_st, h_f)[m // 4][:].rearrange("p a b -> p (a b)").rearrange("p (c n) -> p c n", c=NC)
                for c in range(NC):
                    last = mm(gen_b[0][:, m * B:(m + 1) * B], w[:, c, (m % 4) * P:(m % 4 + 1) * P], cond_s[:, c, :],
                              start=(c == 0), stop=(c == NC - 1))
            last.then_inc(gb_product, 1)
            pe.wait_ge(gb_ready, 12)
            pe.wait_ge(const_ready, 5)
            pe.wait_ge(w_lo_ready, len(names))

            def body(turn, has):
                A, Bb, C = turn, turn + -1, turn + -2

                def project_qk(t):
                    if t == 0:
                        pe.wait_ge(*tlo_done["A"].at(A))
                    split_product(gen(f"Aqk{t}", turn),
                                  three(t_hi["A"], t_lo["A"], wqkv_, slice(t * P, (t + 1) * P), slice(0, 2 * D), NC))\
                        .then_inc(a_proj.sem, 1)

                if "A" in has:
                    norm_transpose("A", turn)
                if "B" in has:
                    pe.wait_ge(*ctx_loaded.at(Bb))
                    o = gen("BctxT", turn)
                    for c in range(NC):
                        last = tr(o[:, c * LC:(c + 1) * LC], ctx_in[:, c * P:(c + 1) * P], ident[0:LC, 0:LC])
                    last.then_inc(ctx_t.sem, 1)
                if "T" in has:
                    output_natural("T", "B", turn)
                if "A" in has:
                    project_qk(0)
                if "T" in has:
                    output_transpose("T", "B", turn)
                if "A" in has:
                    project_qk(1)
                if "T" in has:
                    output_product("T", "B", turn)
                if "A" in has:
                    o = gen("Av", turn)
                    for t in range(NT):
                        last = split_product(o[:, t * D:(t + 1) * D],
                                             three(t_hi["A"], t_lo["A"], wqkv_, slice(t * P, (t + 1) * P),
                                                   slice(2 * D, 3 * D), NC))
                    last.then_inc(a_proj.sem, 1)
                if "B" in has:
                    norm_transpose("B", turn)
                    pe.wait_ge(*ctx_lo.at(Bb))
                    split_product(gen("Bkv", turn)[0:LC, :],
                                  three(c_hi, c_lo, wkv_, slice(0, LC), slice(0, 2 * D), NC)).then_inc(b_kv.sem, 1)
                    pe.wait_ge(*tlo_done["B"].at(Bb))
                    o = gen("Bq", turn)
                    for t in range(NT):
                        last = split_product(o[:, t * D:(t + 1) * D],
                                             three(t_hi["B"], t_lo["B"], wq_, slice(t * P, (t + 1) * P),
                                                   slice(0, D), NC))
                    last.then_inc(b_q.sem, 1)
                if "C" in has:
                    norm_transpose("C", turn)

                def stack_a(k):
                    if k == 0:
                        pe.wait_ge(*nlo_done["A"].at(A))
                    nat_ = q_nat if k < A_STACKS // 2 else k_nat
                    p0 = 2 * (k % (A_STACKS // 2))
                    stack_transposes("A", turn, k, [(a * L + t * P, pair_of(nat_, t, p0 + a), P)
                                                    for a in range(2) for t in range(NT)])
                for k in range(NF // 2):
                    if "A" in has:
                        stack_a(2 * k)
                    if "C" in has:
                        if k == 0:
                            pe.wait_ge(*tlo_done["C"].at(C))
                        o = gen(f"Cf{k}", turn)
                        for j in range(2):
                            f = 2 * k + j
                            last = split_product(o[:, j * L:(j + 1) * L],
                                                 [(w_[:, c, f * P:(f + 1) * P], x_[:, c, :]) for c in range(NC)
                                                  for w_, x_ in ((w1_[0], t_hi["C"]), (w1_[0], t_lo["C"]),
                                                                 (w1_[1], t_hi["C"]))])
                        last.then_inc(f1.sem, 1)
                    if "A" in has:
                        stack_a(2 * k + 1)
                if "A" in has:
                    pe.wait_ge(*st_done["A"].at(A))
                if "C" in has:
                    o = gen("Cout", turn)
                    second = [(o[:, t * D:(t + 1) * D], h_[:, f, t * P:(t + 1) * P], w_[:, f, :], t, f, n)
                              for t in range(NT) for f in range(NF)
                              for n, (h_, w_) in enumerate(((h_hi, w2_[0]), (h_lo, w2_[0]), (h_hi, w2_[1])))]
                for k in range(A_MAX):
                    if "A" in has:
                        scores_a(turn, k)
                    if "C" in has:
                        for o_, l, r, t, f, n in second[3 * k:3 * k + 3]:
                            if t == 0 and f % 2 == 0 and n == 0:
                                pe.wait_ge(*hlo_done.at(C, f // 2 + 1))
                            last = mm(o_, l, r, start=(f == 0 and n == 0), stop=(f == NF - 1 and n == 2))
                if "C" in has:
                    last.then_inc(proj_out["C"].sem, 1)
                if "B" in has:
                    pe.wait_ge(*nlo_done["B"].at(Bb))
                    for k in range(NPAIR // 2):
                        stack_transposes("B", turn, k, [(a * L + t * P, pair_of(q_nat, t, 2 * k + a), P)
                                                        for a in range(2) for t in range(NT)])
                    for k in range(2):
                        stack_transposes("B", turn, NPAIR // 2 + k,
                                         [(a * P, pair_of(k_nat, 0, 4 * k + a, LCE), LCE) for a in range(4)])
                if "A" in has:
                    max_transpose("A", turn)
                if "B" in has:
                    pe.wait_ge(*st_done["B"].at(Bb))
                    for k in range(B_MAX):
                        scores_b(turn, k)
                if "A" in has:
                    pe.wait_ge(*m_rows["A"].at(A))
                    for h in range(A_EXP):
                        shifted_a(turn, h)
                        if h % GRP == 1 and h > GRP:
                            weighted("A", turn, h // GRP - 1)
                        if h == 3 and "B" in has:
                            max_transpose("B", turn)
                    weighted("A", turn, NG - 1)
                elif "B" in has:
                    max_transpose("B", turn)
                if "B" in has:
                    pe.wait_ge(*m_rows["B"].at(Bb))
                    shifted_b(turn, 0)
                    shifted_b(turn, 1)
                if "A" in has:
                    output_natural("A", "A", turn)
                if "B" in has:
                    shifted_b(turn, 2)
                    shifted_b(turn, 3)
                    weighted("B", turn, 0)
                if "A" in has:
                    output_transpose("A", "A", turn)
                if "B" in has:
                    shifted_b(turn, 4)
                    shifted_b(turn, 5)
                    weighted("B", turn, 1)
                if "A" in has:
                    output_product("A", "A", turn)
                if "B" in has:
                    shifted_b(turn, 6)
                    shifted_b(turn, 7)
                    weighted("B", turn, 2)
                    weighted("B", turn, 3)
            run_turns(pe, [gen_use, max_use, exp_use, pv_use], body)


_OUT = ((B, L, D), "float32")


def kernel(**inputs):
    import numpy as np
    import concourse.bacc as bacc
    from concourse.bass_utils import run_bass_kernel_spmd

    f = {k: np.asarray(v) for k, v in inputs.items()}
    w = {k[len("L0_xcond_"):]: v for k, v in f.items() if k.startswith("L0_xcond_")}
    half = DH // 2
    inv_freq = (np.float32(1.0) / np.float32(10000.0) ** (np.arange(half, dtype=np.float32) / np.float32(half)))
    ang = np.arange(L, dtype=np.float32)[:, None] * inv_freq.astype(np.float32)[None, :]
    rope = np.concatenate([np.cos(ang), np.sin(ang), -np.sin(ang)], axis=1).astype(np.float32)
    arrays = {
        "x": f["x"], "ctx": f["ctx_1024"], "cond_t": f["cond_1024"].T, "rope": rope,
        "wqkv": w["qkv_w"].T, "wsa": w["sa_out_w"].T, "wq": w["q_w"].T,
        "wkv": np.concatenate([w["k_w"].T, w["v_w"].T], axis=1), "wca": w["ca_out_w"].T,
        "w1": w["ffn_w1"].T, "w2": w["ffn_w2"].T,
        "lnw": np.stack([w[f"ln{k}_w"].T for k in (1, 2, 3)]),
        "lnb": np.concatenate([w[f"ln{k}_b"].reshape(4, P).T for k in (1, 2, 3)], axis=1),
        "b1": w["ffn_b1"].reshape(NF, P).T, "b2": w["ffn_b2"],
    }
    nc = bacc.Bacc("TRN2", target_bir_lowering=False, num_devices=1)
    host, args = {}, []
    for name, a in arrays.items():
        a = np.ascontiguousarray(a)
        host[f"in_{name}"] = a
        args.append(nc.dram_tensor(f"in_{name}", a.shape, mybir.dt.from_np(a.dtype), kind="ExternalInput").ap())
    args.append(nc.dram_tensor("out_x", _OUT[0], mybir.dt.float32, kind="ExternalOutput").ap())
    layer_kernel(nc, *args)
    r = run_bass_kernel_spmd(nc, [host], core_ids=[0])
    return r.results[0]["out_x"]
```

```python
from contextlib import ExitStack

import concourse.bass as bass
from concourse import mybir

B, L, D, H, DH, DFF, LC = 32, 256, 256, 16, 16, 1024, 77
P = 128
NT = L // P
NC = D // P
NF = DFF // P
NPAIR = H // 2
SROW = P // 2
NS = 3 * DH
NSM = NS + 2
VW = 32
GRP = P // VW
NG = H // GRP
LCE = LC + LC % 2
EPS = 1e-5
SCALE = 1.0 / DH ** 0.5
A_STACKS = NPAIR
B_STACKS = NPAIR // 2 + 2
A_MAX, B_MAX = NT * NPAIR, NT * NPAIR // 2
A_EXP, B_EXP = H, H // 2
NSLOT = 8
PHASE = {"L": 2, "N": 1, "A": 0, "B": -1, "T": -2, "F": -3}
FIRST_LOOP, END_LOOP = 4, B - 2


class Batch:

    def __init__(self, reg, off):
        self.reg, self.off = reg, off

    def __add__(self, n):
        return Batch(self.reg, self.off + n)

    def times(self, per, k=0):
        c = self.off * per + k
        if self.reg is None:
            return c
        v = self.reg * per if per != 1 else self.reg
        return v + c if c else v


class Event:

    def __init__(self, sem, per, inc, held):
        self.sem, self.per, self.inc, self.held = sem, per, inc, held

    def at(self, batch, k=None):
        if batch.reg is None and batch.off > B - 1:
            batch, k = Batch(None, B - 1), None
        v = batch.times(self.per * self.inc, self.inc * (self.per if k is None else k))
        return self.held if isinstance(v, int) and v <= 0 else (self.sem, v)


class Reuse:

    def __init__(self, held, uses):
        self.held = held
        self.uses = {u[0]: u for u in uses}
        self.last_of_turn = {u[1]: u for u in uses}
        self.last = {}

    def before(self, name, batch):
        _, slot, _, _ = use = self.uses[name]
        end = self.held
        if slot in self.last:
            (_, _, event, k), before = self.last[slot]
            end = event.at(before, k)
        self.last[slot] = (use, batch)
        return end

    def turn_before(self, turn):
        self.last = {s: (u, turn + (PHASE[u[0][0]] - 1)) for s, u in self.last_of_turn.items()}


def of_batch(step):
    def run(batch, *args):
        if batch is not None:
            step(batch, *args)
    return run


def run_turns(eng, reuses, body):
    def peeled(t):
        body(*(Batch(None, t + off) if 0 <= t + off < B else None for off in PHASE.values()))
    for t in range(-1, FIRST_LOOP):
        peeled(t)
    with eng.Fori(FIRST_LOOP, END_LOOP) as i:
        for r in reuses:
            r.turn_before(Batch(i, 0))
        body(*(Batch(i, off) for off in PHASE.values()))
    for r in reuses:
        r.turn_before(Batch(None, END_LOOP))
    for t in range(END_LOOP, B + 3):
        peeled(t)


def layer_kernel(nc, x, ctx, cond_t, rope, wqkv, wsa, wq, wkv, wca, w1, w2, lnw, lnb, b1, b2, out):
    f32, f32r = mybir.dt.float32, mybir.dt.float32r
    ALU, ACT, AX = mybir.AluOpType, mybir.ActivationFunctionType, mybir.AxisListType
    x_d = x.rearrange("b (t p) d -> b p t d", p=P)
    out_d = out.rearrange("b (t p) d -> b p t d", p=P)

    with ExitStack() as es:
        def sb(name, shape, dt=f32):
            return es.enter_context(nc.sbuf_tensor(name, shape, dt))

        def sem(name):
            return es.enter_context(nc.semaphore(name))

        def event(name, per, inc=1):
            return Event(sem(name), per, inc, HELD)

        names = [("qkv", NC * 3 * D, wqkv), ("sa", NC * D, wsa), ("q", NC * D, wq), ("kv", NC * 2 * D, wkv),
                 ("w1", NC * DFF, w1), ("w2", NF * D, w2), ("ca", NC * D, wca)]
        w_at, total = {}, 0
        for n, cols, _ in names:
            w_at[n] = (total, cols)
            total += cols
        w_hi, w_lo = sb("w_hi", [P, total], f32r), sb("w_lo", [P, total], f32r)

        def weight(name, chunks):
            a, cols = w_at[name]
            return (w_hi[:, a:a + cols].rearrange("p (c n) -> p c n", c=chunks),
                    w_lo[:, a:a + cols].rearrange("p (c n) -> p c n", c=chunks))

        ident, ident_r = sb("ident", [P, P]), sb("ident_r", [P, P], f32r)
        rope_t = sb("rope_t", [P, NT, 3, 8])
        gb = sb("gb", [P, 3, 4, B])
        lnb_t = sb("lnb_t", [P, 12])
        b1_t, b2_t = sb("b1_t", [P, NF]), sb("b2_t", [P, D])
        minus_half = sb("minus_half", [P, NT])
        fence = {s: sb(f"fence_{s}", [P, 1]) for s in "ABC"}
        pool_fence = sb("pool_fence", [P, 32])
        cond_s = sb("cond_s", [P, NC, B])
        x_in, xa, xt, xc = (sb(n, [P, NT, D]) for n in ("x_in", "xa", "xt", "xc"))
        ctx_in = sb("ctx_in", [LC, D])
        xn = sb("xn", [P, NT, D])
        stats = {s: sb(f"stats_{s}", [P, NT, 6]) for s in "ABC"}
        mv = {s: sb(f"mv_{s}", [P, NT, 2]) for s in "ABC"}
        ve = {s: sb(f"ve_{s}", [P, NT]) for s in "ABC"}
        rstd = {s: sb(f"rstd_{s}", [P, NT]) for s in "ABC"}
        t_f = sb("t_f", [P, NC, L])
        t_hi = {s: sb(f"t_hi_{s}", [P, NC, L], f32r) for s in "ABC"}
        t_lo = {s: sb(f"t_lo_{s}", [P, NC, L], f32r) for s in "ABC"}
        c_hi, c_lo = sb("c_hi", [P, NC, LC], f32r), sb("c_lo", [P, NC, LC], f32r)
        rot_c = sb("rot_c", [P, NT, 2 * D])
        rot_s = sb("rot_s", [P, 2 * D])
        rk_c, rk_s = sb("rk_c", [LC, D]), sb("rk_s", [LC, D])
        q_nat = sb("q_nat", [P, NT, H, SROW], f32r)
        k_nat = sb("k_nat", [P, NT, H, SROW], f32r)
        q_st = {s: sb(f"q_st_{s}", [P, NPAIR, L], f32r) for s in "AB"}
        k_st_a = sb("k_st_a", [P, NPAIR, L], f32r)
        k_st_b = sb("k_st_b", [P, NPAIR, 2, P], f32r)
        v_a = sb("v_a", [P, NT, H, VW])
        v_b = sb("v_b", [LC, H, VW])
        mx = {s: sb(f"mx_{s}", [P, NT, H]) for s in "AB"}
        nm = {s: sb(f"nm_{s}", [P, NT, 2, 2, NPAIR], f32r) for s in "AB"}
        m_rows_t = sb("m_rows_t", [4 * H, L], f32r)
        m_t = {"A": m_rows_t[0:2 * H, :], "B": m_rows_t[2 * H:4 * H, :]}
        probs = sb("probs", [P, NSLOT, 2 * L])
        o_st = sb("o_st", [P, 2, 2 * L])
        rden = sb("rden", [P, NT, H])
        o_n = sb("o_n", [P, NT, D])
        o_hi, o_lo = sb("o_hi", [P, NC, L], f32r), sb("o_lo", [P, NC, L], f32r)
        h_f = sb("h_f", [P, 2, 2 * L])
        h_hi, h_lo = sb("h_hi", [P, NF, L], f32r), sb("h_lo", [P, NF, L], f32r)

        psum = {}
        for name in ("gen", "maxs", "exps", "pvs"):
            pair = es.enter_context(nc.psum_tensor(name, [P, 2 * 512], f32))
            psum[name, 0], psum[name, 1] = pair[:, 0:512], pair[:, 512:1024]

        ld_const, ld_w = sem("ld_const"), [sem("ld_w0"), sem("ld_w1")]
        w_hi_ready, w_lo_ready = sem("w_hi_ready"), sem("w_lo_ready")
        pool_zeroed, const_ready = sem("pool_zeroed"), sem("const_ready")
        gb_product, gb_ready = sem("gb_product"), sem("gb_ready")
        HELD = (w_hi_ready, 1)

        x_loaded, ctx_loaded, out_stored = (event(n, 1, 16) for n in ("x_loaded", "ctx_loaded", "out_stored"))
        xa_loaded, xt_copied, xc_made = event("xa_loaded", 1, 16), event("xt_copied", 1), event("xc_made", 1)

        def per_layer(what, stages, per, inc=1):
            return {s: event(f"{s}_{what}", per[s] if isinstance(per, dict) else per, inc) for s in stages}

        stat_done, mv_done, var_done = (per_layer(n, "ABC", k) for n, k in (("stat", NT), ("mv", NT), ("var", 1)))
        rstd_done, xn_done, ln_t = (per_layer(n, "ABC", k) for n, k in (("rstd", 1), ("xn", NT), ("lnT", 1)))
        t_done, thi_done, tlo_done = (per_layer(n, "ABC", k) for n, k in (("t", NC), ("thi", 1), ("tlo", 1)))
        ctx_t, ctx_hi, ctx_lo = event("ctx_t", 1), event("ctx_hi", 1), event("ctx_lo", 1)
        a_proj, b_kv, b_q = event("a_proj", NT + 1), event("b_kv", 1), event("b_q", 1)
        v_ready = per_layer("v", "AB", 1)
        TILES = {"A": NT, "B": NT + 1}
        cos_done, sin_done = (per_layer(n, "AB", TILES) for n in ("cos", "sin"))
        rot_done = per_layer("rot", "AB", {s: 2 * n for s, n in TILES.items()})
        PIECES = {"A": 2 * NT, "B": NT + 1}
        nhi_done = per_layer("nhi", "AB", PIECES)
        nlo_done = per_layer("nlo", "AB", PIECES)
        STACKS, MAXES, EXPS = ({"A": a, "B": b} for a, b in ((A_STACKS, B_STACKS), (A_MAX, B_MAX), (A_EXP, B_EXP)))
        st_t = per_layer("stT", "AB", STACKS)
        qst_done = per_layer("qst", "AB", NPAIR // 2)
        kst_done = per_layer("kst", "AB", NPAIR // 2)
        score, mx_done = per_layer("score", "AB", MAXES), per_layer("mx", "AB", MAXES)
        nmhi_done, nm_done = per_layer("nmhi", "AB", NT), per_layer("nm", "AB", NT)
        m_tr, m_copied, m_rows = (per_layer(n, "AB", 1) for n in ("mT", "mcopy", "mrows"))
        m_rows = {s: Event(e.sem, 4, 16, HELD) for s, e in m_rows.items()}
        shifted, p_done = per_layer("shifted", "AB", EXPS), per_layer("p", "AB", EXPS)
        pv, o_copied = per_layer("pv", "AB", NG), per_layer("ocopy", "AB", 2)
        o_nat, rden_done, on_done = (per_layer(n, "AB", NT) for n in ("onat", "rden", "on"))
        o_tr, ohi_done, olo_done = (per_layer(n, "AB", 1) for n in ("oT", "ohi", "olo"))
        proj_out = per_layer("proj", "ABC", 1)
        res_done = per_layer("res", "ABC", 1)
        f1, gelu_done = event("f1", NF // 2), event("gelu", NF)
        hhi_done, hlo_done = event("hhi", NF // 2), event("hlo", NF // 2)

        bank_uses = [("Fout", ("gen", 0), res_done["C"], 1),
                     ("BlnT", ("gen", 1), t_done["B"], NC),
                     ("NlnT", ("gen", 1), t_done["A"], NC),
                     ("Bkv", ("gen", 1), v_ready["B"], 1)]
        for k in range(NPAIR // 2):
            bank_uses += [(f"Aqst{k}", ("exps", 0), qst_done["A"], k + 1),
                          (f"Akst{k}", ("exps", 1), kst_done["A"], k + 1)]
        bank_uses += [(f"Ascore{k}", ("maxs", k % 2), mx_done["A"], k + 1) for k in range(A_MAX)]
        bank_uses += [(f"Tshift{k}", ("exps", k % 2), p_done["B"], k + 1) for k in range(B_EXP)]
        bank_uses += [(f"Tpv{k}", ("pvs", k), o_copied["B"], k + 1) for k in range(2)]
        bank_uses += [("AmT", ("maxs", 0), m_copied["A"], 1),
                      ("Ton0", ("exps", 0), on_done["B"], 1), ("Ton1", ("exps", 1), on_done["B"], 2),
                      ("Bq", ("pvs", 0), sin_done["B"], NT + 1),
                      ("ToT", ("maxs", 1), olo_done["B"], 1),
                      ("Tout", ("maxs", 0), res_done["B"], 1)]
        bank_uses += [(f"Ashift{k}", ("exps", k % 2), p_done["A"], k + 1) for k in range(A_EXP)]
        bank_uses += [(f"Apv{k}", ("pvs", k), o_copied["A"], k + 1) for k in range(2)]
        bank_uses += [(f"Bkst{k}", ("gen", k % 2), kst_done["B"], 2 * k + 2) for k in range(2)]
        bank_uses += [(f"Bqst{k}", ("gen", k % 2), qst_done["B"], k + 1) for k in range(NPAIR // 2)]
        bank_uses += [("ActxT", ("maxs", 1), ctx_lo, 1)]
        bank_uses += [(f"Bscore{k}", ("maxs", k % 2), mx_done["B"], k + 1) for k in range(B_MAX)]
        bank_uses += [("TlnT", ("gen", 0), t_done["C"], NC),
                      ("Nqk0", ("gen", 1), sin_done["A"], 1), ("Nqk1", ("gen", 0), sin_done["A"], 2),
                      ("BmT", ("maxs", 0), m_copied["B"], 1)]
        bank_uses += [(f"Tf{k}", ("maxs", 1 - k % 2), gelu_done, 2 * k + 2) for k in range(NF // 2)]
        bank_uses += [("Aon0", ("exps", 0), on_done["A"], 1), ("Aon1", ("exps", 1), on_done["A"], 2),
                      ("AoT", ("exps", 0), olo_done["A"], 1),
                      ("Aout", ("exps", 1), res_done["A"], 1),
                      ("Nv", ("gen", 1), v_ready["A"], 1)]
        bank_of = {name: where for name, where, _, _ in bank_uses}

        def bank(name):
            return psum[bank_of[name]]

        def halves(t):
            return t[:].rearrange("p c n -> p (c n)")

        block = es.enter_context(nc.Block())

        @block.sync
        def _(sp):
            def const(dst, src):
                sp.dma_start(dst, src).then_inc(ld_const, 16)

            const(cond_s[:], cond_t.rearrange("(c p) b -> p c b", p=P))
            for k, t in enumerate((rot_c, o_st, h_f)):
                const(t[:].rearrange("p a b -> p (a b)").rearrange("p (c n) -> p c n", c=NC),
                      lnw[k].rearrange("(c p) n -> p c n", p=P))
            const(lnb_t[:], lnb)
            const(rope_t[:].rearrange("p t k d -> p t (k d)"), rope.rearrange("(t p) n -> p t n", p=P))
            const(b1_t[:], b1)
            const(b2_t[:], b2[None, :].to_broadcast([P, D]))
            sp.dma_start(x_in[:], x_d[0]).then_inc(x_loaded.sem, 16)
            for k, (n, cols, src) in enumerate(names):
                if k >= 2:
                    sp.wait_ge(w_lo_ready, k - 1)
                stage = probs[:, 4 * (k % 2):4 * (k % 2) + 4, :].rearrange("p a b -> p (a b)")[:, 0:cols]
                sp.dma_start(stage.rearrange("p (c n) -> p c n", c=src.shape[0] // P),
                             src.rearrange("(c p) n -> p c n", p=P)).then_inc(ld_w[k % 2], 16)

            @of_batch
            def max_rows(bt, s):
                sp.wait_ge(*m_copied[s].at(bt))
                for par in range(2):
                    for j in range(2):
                        row, r0 = SROW * par + NS + j, (par * 2 + j) * NPAIR
                        sp.dma_start(q_st[s][row:row + 1, :, :].bitcast(f32),
                                     m_t[s][r0:r0 + NPAIR, :].bitcast(f32)).then_inc(m_rows[s].sem, 16)

            @of_batch
            def load_input(bt):
                sp.wait_ge(*xn_done["A"].at(bt + -1))
                sp.dma_start(x_in[:], x_d[bt.times(1)]).then_inc(x_loaded.sem, 16)

            @of_batch
            def store(bt):
                sp.wait_ge(*res_done["C"].at(bt))
                sp.dma_start(out_d[bt.times(1)], xc[:]).then_inc(out_stored.sem, 16)

            @of_batch
            def load(bt):
                sp.wait_ge(*ctx_t.at(bt + -1))
                sp.dma_start(ctx_in[:], ctx[bt.times(1)]).then_inc(ctx_loaded.sem, 16)
                sp.wait_ge(*xt_copied.at(bt + -1))
                sp.dma_start(xa[:], x_d[bt.times(1)]).then_inc(xa_loaded.sem, 16)

            def body(L_, N, A, B_, T, F):
                load_input(L_)
                max_rows(A, "A")
                store(F)
                load(A)
                max_rows(B_, "B")
            run_turns(sp, [], body)
            sp.wait_ge(out_stored.sem, 16 * B)

        @block.gpsimd
        def _(pool):
            g = nc.gpsimd
            v_a_ht = v_a[:].rearrange("p t h w -> p (t h) w")
            k_nat_ht = k_nat[:].rearrange("p t h w -> p (t h) w")
            g.memset(ident[:], 0.0).then_inc(pool_zeroed, 1)
            g.memset(minus_half[:], -0.5).then_inc(const_ready, 1)
            g.memset(v_a_ht[:, :, DH:VW], 0.0).then_inc(pool_zeroed, 1)
            g.memset(v_b[:, :, DH:VW], 0.0).then_inc(pool_zeroed, 1)
            g.memset(q_nat[:].bitcast(f32), 0.0).then_inc(pool_zeroed, 1)
            g.memset(k_nat[:].bitcast(f32), 0.0).then_inc(pool_zeroed, 1)
            g.memset(k_st_b[:].bitcast(f32), 0.0).then_inc(pool_zeroed, 1)
            pool.wait_ge(pool_zeroed, 6)
            g.affine_select(out=ident[:], in_=ident[:], compare_op=ALU.not_equal, fill=1.0, base=0,
                            pattern=[[-1, P]], channel_multiplier=1).then_inc(pool_zeroed, 1)
            g.memset(v_a_ht[:, :, DH:DH + 1], 1.0).then_inc(const_ready, 1)
            g.memset(v_b[:, :, DH:DH + 1], 1.0).then_inc(const_ready, 1)
            g.memset(k_nat_ht[:, :, NS:NSM].bitcast(f32), 1.0).then_inc(const_ready, 1)
            pool.wait_ge(pool_zeroed, 7)
            g.tensor_copy(ident_r[:], ident[:]).then_inc(const_ready, 1)
            for k, (n, cols, _) in enumerate(names):
                a = w_at[n][0]
                pool.wait_ge(w_hi_ready, k + 1)
                stage = probs[:, 4 * (k % 2):4 * (k % 2) + 4, :].rearrange("p a b -> p (a b)")[:, 0:cols]
                g.tensor_tensor(w_lo[:, a:a + cols], stage, w_hi[:, a:a + cols].bitcast(f32), ALU.subtract)\
                    .then_inc(w_lo_ready, 1)

            @of_batch
            def power(bt, s):
                pool.wait_ge(*var_done[s].at(bt))
                pool.wait_ge(*xn_done[s].at(bt + -1))
                g.tensor_tensor(rstd[s][:], ve[s][:], minus_half[:], ALU.pow).then_inc(rstd_done[s].sem, 1)

            @of_batch
            def residual_and_bias(bt):
                pool.wait_ge(*xn_done["C"].at(bt))
                pool.wait_ge(*out_stored.at(bt + -1))
                g.tensor_tensor(xc[:], xt[:], b2_t[:, None, :].to_broadcast([P, NT, D]), ALU.add)\
                    .then_inc(xc_made.sem, 1)

            @of_batch
            def move_residual(bt):
                pool.wait_ge(*xn_done["B"].at(bt))
                pool.wait_ge(*xc_made.at(bt + -1))
                g.tensor_tensor(pool_fence[:, 0:1], minus_half[:, 0:1], minus_half[:, 0:1], ALU.mult)
                g.tensor_copy(xt[:], xa[:]).then_inc(xt_copied.sem, 1)

            @of_batch
            def gelu_low(bt, k):
                pool.wait_ge(*hhi_done.at(bt, k + 1))
                if k == 0:
                    pool.wait_ge(*proj_out["C"].at(bt + -1))
                g.tensor_tensor(h_lo[:, 2 * k:2 * k + 2, :], h_f[:, k % 2, :].rearrange("p (c n) -> p c n", c=2),
                                h_hi[:, 2 * k:2 * k + 2, :].bitcast(f32), ALU.subtract).then_inc(hlo_done.sem, 1)

            def body(L_, N, A, B_, T, F):
                power(N, "A")
                power(T, "C")
                residual_and_bias(T)
                move_residual(B_)
                gelu_low(T, 0)
                gelu_low(T, 1)
                power(A, "B")
                gelu_low(T, 2)
                gelu_low(T, 3)
            run_turns(pool, [], body)

        @block.scalar
        def _(act):
            s_ = nc.scalar
            t_use = Reuse(HELD, [("B", 0, tlo_done["B"], 1), ("N", 0, tlo_done["A"], 1), ("T", 0, tlo_done["C"], 1)])
            p_use = Reuse(HELD, [(f"T{k}", k, pv["B"], k // 2 + 1) for k in range(B_EXP)]
                          + [(f"A{h}", h % NSLOT, pv["A"], h // GRP + 1) for h in range(A_EXP)])
            o_use = Reuse(HELD, [(f"T{k}", k, o_nat["B"], NT) for k in range(2)]
                          + [(f"A{k}", k, o_nat["A"], NT) for k in range(2)])
            oh_use = Reuse(HELD, [("T", 0, proj_out["B"], 1), ("A", 0, proj_out["A"], 1)])
            nat_use = Reuse(HELD, [("B", 0, st_t["B"], B_STACKS), ("N", 0, st_t["A"], A_STACKS)])
            h_use = Reuse(HELD, [(f"T{k}", k % 2, hlo_done, k + 1) for k in range(NF // 2)])

            def column(ln, c, bt):
                return gb[:, ln, c, bt.off:bt.off + 1] if bt.reg is None else gb[:, ln, c, bass.ds(bt.times(1), 1)]

            @of_batch
            def modulate(bt, phase, s):
                ln = "ABC".index(s)
                act.wait_ge(*ln_t[s].at(bt))
                act.wait_ge(*t_use.before(phase, bt))
                for c in range(NC):
                    s_.activation(t_f[:, c, :], bank(phase + "lnT")[:, c * L:(c + 1) * L], ACT.Identity,
                                  scale=column(ln, c, bt), bias=column(ln, NC + c, bt)).then_inc(t_done[s].sem, 1)

            @of_batch
            def context_high(bt):
                act.wait_ge(*ctx_t.at(bt))
                act.wait_ge(*b_kv.at(bt + -1))
                s_.activation(halves(c_hi), bank("ActxT")[:, 0:NC * LC], ACT.Copy).then_inc(ctx_hi.sem, 1)

            @of_batch
            def values_self(bt):
                act.wait_ge(*a_proj.at(bt, NT + 1))
                act.wait_ge(*pv["A"].at(bt + -1))
                s_.activation(v_a[:].rearrange("p t h w -> p (t h) w")[:, :, 0:DH],
                              bank("Nv").rearrange("p (a d) -> p a d", d=DH), ACT.Copy).then_inc(v_ready["A"].sem, 1)

            @of_batch
            def values_cross(bt):
                act.wait_ge(*b_kv.at(bt))
                act.wait_ge(*sin_done["B"].at(bt, 1))
                act.wait_ge(*pv["B"].at(bt + -1))
                s_.activation(v_b[:, :, 0:DH], bank("Bkv")[0:LC, D:2 * D].rearrange("p (h d) -> p h d", d=DH),
                              ACT.Copy).then_inc(v_ready["B"].sem, 1)

            def stack_high(s, src, dst, blocks):
                out_ = dst[:, :, 0:NS].rearrange("p h (b d) -> p h b d", d=DH)[:, :, blocks, :]
                s_.activation(out_, src.rearrange("p (h d) -> p h d", d=DH)[:, :, None, :]
                              .to_broadcast([out_.shape[0], H, 2, DH]), ACT.Copy).then_inc(nhi_done[s].sem, 1)

            @of_batch
            def stacks_high_self(bt, t):
                act.wait_ge(*rot_done["A"].at(bt, 2 * t + 2))
                if t == 0:
                    act.wait_ge(*nat_use.before("N", bt))
                stack_high("A", rot_c[:, t, 0:D], q_nat[:, t], slice(0, 3, 2))
                stack_high("A", rot_c[:, t, D:2 * D], k_nat[:, t], slice(0, 2))

            @of_batch
            def stack_high_cross(bt, k):
                act.wait_ge(*rot_done["B"].at(bt, 2 * k + 2))
                if k == 0:
                    act.wait_ge(*nat_use.before("B", bt))
                    stack_high("B", rk_c[:, :], k_nat[0:LC, 0], slice(0, 2))
                else:
                    stack_high("B", rot_c[:, k - 1, 0:D], q_nat[:, k - 1], slice(0, 3, 2))

            @of_batch
            def stacks_self(bt, k):
                act.wait_ge(*st_t["A"].at(bt, 2 * k + 1))
                if k == 0:
                    act.wait_ge(*shifted["A"].at(bt + -1))
                s_.activation(q_st["A"][:, 2 * k:2 * k + 2, :], bank(f"Aqst{k}").rearrange("p (a n) -> p a n", a=2),
                              ACT.Copy).then_inc(qst_done["A"].sem, 1)
                act.wait_ge(*st_t["A"].at(bt, 2 * k + 2))
                s_.activation(k_st_a[:, 2 * k:2 * k + 2, :], bank(f"Akst{k}").rearrange("p (a n) -> p a n", a=2),
                              ACT.Copy).then_inc(kst_done["A"].sem, 1)

            @of_batch
            def stack_q_cross(bt, k):
                act.wait_ge(*st_t["B"].at(bt, 2 + k + 1))
                if k == 0:
                    act.wait_ge(*shifted["B"].at(bt + -1))
                s_.activation(q_st["B"][:, 2 * k:2 * k + 2, :], bank(f"Bqst{k}").rearrange("p (a n) -> p a n", a=2),
                              ACT.Copy).then_inc(qst_done["B"].sem, 1)

            @of_batch
            def max_rows(bt, s):
                act.wait_ge(*m_tr[s].at(bt))
                act.wait_ge(*m_rows[s].at(bt + -1))
                s_.activation(m_t[s], bank(s + "mT")[0:2 * H, 0:L], ACT.Copy).then_inc(m_copied[s].sem, 1)

            @of_batch
            def exps(bt, phase, s, k, rows):
                act.wait_ge(*shifted[s].at(bt, k + 1))
                act.wait_ge(*p_use.before(f"{phase}{k}", bt))
                s_.activation(probs[0:rows, k % NSLOT, :], bank(f"{phase}shift{k}")[0:rows, :], ACT.Exp,
                              scale=SCALE).then_inc(p_done[s].sem, 1)

            @of_batch
            def outputs(bt, phase, s, k):
                act.wait_ge(*pv[s].at(bt, 2 * k + 2))
                act.wait_ge(*o_use.before(f"{phase}{k}", bt))
                s_.activation(o_st[:, k, :], bank(f"{phase}pv{k}"), ACT.Copy).then_inc(o_copied[s].sem, 1)

            @of_batch
            def output_high(bt, phase, s):
                act.wait_ge(*o_tr[s].at(bt))
                act.wait_ge(*oh_use.before(phase, bt))
                s_.activation(halves(o_hi), bank(phase + "oT"), ACT.Copy).then_inc(ohi_done[s].sem, 1)

            @of_batch
            def gelu(bt, k):
                act.wait_ge(*f1.at(bt, k + 1))
                act.wait_ge(*h_use.before(f"T{k}", bt))
                for j in range(2):
                    s_.activation(h_f[:, k % 2, j * L:(j + 1) * L], bank(f"Tf{k}")[:, j * L:(j + 1) * L],
                                  ACT.Gelu, bias=b1_t[:, 2 * k + j:2 * k + j + 1]).then_inc(gelu_done.sem, 1)

            act.wait_ge(gb_ready, 12)
            act.wait_ge(const_ready, 5)
            act.wait_ge(w_lo_ready, len(names))

            def body(L_, N, A, B_, T, F):
                stacks_self(A, 0)
                stacks_self(A, 1)
                stacks_self(A, 2)
                modulate(B_, "B", "B")
                stacks_self(A, 3)
                exps(T, "T", "B", 0, LC)
                exps(T, "T", "B", 1, LC)
                exps(T, "T", "B", 2, LC)
                exps(T, "T", "B", 3, LC)
                modulate(N, "N", "A")
                exps(T, "T", "B", 4, LC)
                exps(T, "T", "B", 5, LC)
                outputs(T, "T", "B", 0)
                exps(T, "T", "B", 6, LC)
                exps(T, "T", "B", 7, LC)
                outputs(T, "T", "B", 1)
                max_rows(A, "A")
                stack_high_cross(B_, 0)
                values_cross(B_)
                stack_high_cross(B_, 1)
                output_high(T, "T", "B")
                for h in range(A_EXP):
                    exps(A, "A", "A", h, P)
                    if h == 1:
                        stack_high_cross(B_, 2)
                    if 5 <= h < 9:
                        stack_q_cross(B_, h - 5)
                    if h == 9:
                        context_high(A)
                    if h == 11:
                        outputs(A, "A", "A", 0)
                    if h == 12:
                        modulate(T, "T", "C")
                outputs(A, "A", "A", 1)
                max_rows(B_, "B")
                gelu(T, 0)
                stacks_high_self(N, 0)
                gelu(T, 1)
                output_high(A, "A", "A")
                stacks_high_self(N, 1)
                gelu(T, 2)
                values_self(N)
                gelu(T, 3)
            run_turns(act, [t_use, p_use, o_use, oh_use, h_use, nat_use], body)

        @block.vector
        def _(dve):
            v = nc.vector
            for k, (n, cols, _) in enumerate(names):
                a = w_at[n][0]
                dve.wait_ge(ld_w[k % 2], 16 * (k // 2 + 1))
                stage = probs[:, 4 * (k % 2):4 * (k % 2) + 4, :].rearrange("p a b -> p (a b)")[:, 0:cols]
                v.tensor_copy(w_hi[:, a:a + cols], stage).then_inc(w_hi_ready, 1)
                if k == 0:
                    dve.wait_ge(gb_product, 1)
                    for m in range(12):
                        v.tensor_scalar(gb[:, m // 4, m % 4, :], psum["gen", 0][:, m * B:(m + 1) * B],
                                        lnb_t[:, m:m + 1], 1.0 if m % 4 < NC else 0.0, ALU.add, ALU.add)\
                            .then_inc(gb_ready, 1)
            dve.wait_ge(gb_ready, 12)

            rot_use = Reuse(HELD, [("B0", 0, nlo_done["B"], 2), ("B1", 1, nlo_done["B"], 3),
                                   ("N0", 0, nlo_done["A"], 2), ("N1", 1, nlo_done["A"], 4)])
            rots_use = Reuse(HELD, [("B0", 0, rot_done["B"], 4), ("B1", 0, rot_done["B"], 6),
                                    ("N0", 0, rot_done["A"], 2), ("N1", 0, rot_done["A"], 4)])
            on_use = Reuse(HELD, [("T", 0, o_tr["B"], 1), ("A", 0, o_tr["A"], 1)])
            ol_use = Reuse(HELD, [("T", 0, proj_out["B"], 1), ("A", 0, proj_out["A"], 1)])
            xn_use = Reuse(HELD, [("N", 0, ln_t["A"], 1), ("T", 0, ln_t["C"], 1), ("A", 0, ln_t["B"], 1)])
            nat_use = Reuse(HELD, [("B", 0, st_t["B"], B_STACKS), ("N", 0, st_t["A"], A_STACKS)])
            norm_used = {"A": a_proj, "B": b_q, "C": f1}

            @of_batch
            def split_norm(bt, s):
                dve.wait_ge(*t_done[s].at(bt))
                dve.wait_ge(*norm_used[s].at(bt + -1))
                v.tensor_copy(t_hi[s][:], t_f[:]).then_inc(thi_done[s].sem, 1)
                dve.wait_ge(*thi_done[s].at(bt))
                v.tensor_tensor(t_lo[s][:], t_f[:], t_hi[s][:].bitcast(f32), ALU.subtract)\
                    .then_inc(tlo_done[s].sem, 1)

            @of_batch
            def context_low(bt):
                dve.wait_ge(*ctx_hi.at(bt))
                dve.wait_ge(*b_kv.at(bt + -1))
                v.tensor_tensor(halves(c_lo), bank("ActxT")[:, 0:NC * LC], halves(c_hi).bitcast(f32), ALU.subtract)\
                    .then_inc(ctx_lo.sem, 1)

            def rotation(s, bt, k, src, cos_out, sin_out, t, rows):
                n = src.shape[-1] // DH
                cosv = rope_t[0:rows, t, None, 0:1, :].to_broadcast([rows, n, 2, 8])
                sinv = rope_t[0:rows, t, None, 1:3, :].to_broadcast([rows, n, 2, 8])
                sv = src.rearrange("p (h s d) -> p h s d", s=2, d=8)
                cv = cos_out.rearrange("p (h s d) -> p h s d", s=2, d=8)
                ov = sin_out.rearrange("p (h s d) -> p h s d", s=2, d=8)
                v.tensor_tensor(cv, sv, cosv, ALU.mult).then_inc(cos_done[s].sem, 1)
                v.tensor_tensor(ov, sv, sinv, ALU.mult).then_inc(sin_done[s].sem, 1)
                dve.wait_ge(*sin_done[s].at(bt, k + 1))
                for half in range(2):
                    v.tensor_tensor(cv[:, :, half, :], cv[:, :, half, :], ov[:, :, 1 - half, :], ALU.add)\
                        .then_inc(rot_done[s].sem, 1)

            @of_batch
            def rotate_self(bt, t):
                dve.wait_ge(*a_proj.at(bt, t + 1))
                dve.wait_ge(*rot_use.before(f"N{t}", bt))
                dve.wait_ge(*rots_use.before(f"N{t}", bt))
                rotation("A", bt, t, bank(f"Nqk{t}"), rot_c[:, t, :], rot_s[:, :], t, P)

            @of_batch
            def rotate_cross_k(bt):
                dve.wait_ge(*b_kv.at(bt))
                rotation("B", bt, 0, bank("Bkv")[0:LC, 0:D], rk_c[:, :], rk_s[:, :], 0, LC)

            @of_batch
            def rotate_cross_q(bt, t):
                if t == 0:
                    dve.wait_ge(*b_q.at(bt))
                dve.wait_ge(*rot_use.before(f"B{t}", bt))
                dve.wait_ge(*rots_use.before(f"B{t}", bt))
                rotation("B", bt, t + 1, bank("Bq")[:, t * D:(t + 1) * D], rot_c[:, t, 0:D], rot_s[:, 0:D], t, P)

            def stack_low(s, bt, k, src, dst, block):
                dve.wait_ge(*nhi_done[s].at(bt, k + 1))
                v.tensor_tensor(dst[:, :, block * DH:(block + 1) * DH], src.rearrange("p (h d) -> p h d", d=DH),
                                dst[:, :, 0:DH].bitcast(f32), ALU.subtract).then_inc(nlo_done[s].sem, 1)

            @of_batch
            def stacks_low_self(bt, t):
                if t == 0:
                    dve.wait_ge(*nat_use.before("N", bt))
                stack_low("A", bt, 2 * t, rot_c[:, t, 0:D], q_nat[:, t], 1)
                stack_low("A", bt, 2 * t + 1, rot_c[:, t, D:2 * D], k_nat[:, t], 2)

            @of_batch
            def stack_low_cross(bt, k):
                if k == 0:
                    dve.wait_ge(*nat_use.before("B", bt))
                    stack_low("B", bt, 0, rk_c[:, :], k_nat[0:LC, 0], 2)
                else:
                    stack_low("B", bt, k, rot_c[:, k - 1, 0:D], q_nat[:, k - 1], 1)

            @of_batch
            def stack_k_cross(bt, k):
                dve.wait_ge(*st_t["B"].at(bt, k + 1))
                if k == 0:
                    dve.wait_ge(*shifted["B"].at(bt + -1))
                for par in range(2):
                    r = slice(SROW * par, SROW * (par + 1))
                    v.tensor_copy(k_st_b[r, 4 * k:4 * k + 4, par, 0:LC],
                                  bank(f"Bkst{k}")[r, :].rearrange("p (a n) -> p a n", a=4)[:, :, 0:LC])\
                        .then_inc(kst_done["B"].sem, 1)

            @of_batch
            def statistics(bt, s, src, ready):
                dve.wait_ge(*ready.at(bt))
                for t in range(NT):
                    v.bn_stats(stats[s][:, t, :], src[:, t, :]).then_inc(stat_done[s].sem, 1)

            @of_batch
            def variance(bt, s):
                dve.wait_ge(*stat_done[s].at(bt))
                v.memset(fence[s][:], 0.0)
                for t in range(NT):
                    v.bn_aggr(mv[s][:, t, :], stats[s][:, t, :]).then_inc(mv_done[s].sem, 1)
                dve.wait_ge(*mv_done[s].at(bt))
                dve.wait_ge(*rstd_done[s].at(bt + -1))
                v.tensor_scalar(ve[s][:], mv[s][:, :, 1], EPS, None, ALU.add).then_inc(var_done[s].sem, 1)

            @of_batch
            def normalise(bt, phase, s, src):
                dve.wait_ge(*rstd_done[s].at(bt))
                dve.wait_ge(*xn_use.before(phase, bt))
                for t in range(NT):
                    v.tensor_scalar(xn[:, t, :], src[:, t, :], mv[s][:, t, 0:1], rstd[s][:, t:t + 1],
                                    ALU.subtract, ALU.mult).then_inc(xn_done[s].sem, 1)

            @of_batch
            def maxima_self(bt, k):
                t, pair, par = k // NPAIR, 2 * (k % NPAIR // 2), k % 2
                dve.wait_ge(*score["A"].at(bt, k + 1))
                if k == 0:
                    dve.wait_ge(*nm_done["A"].at(bt + -1))
                v.reduce_max(mx["A"][:, t, :].rearrange("p (a q) -> p q a", q=2)[:, par, pair:pair + 2],
                             bank(f"Ascore{k}").rearrange("p (a n) -> p a n", a=2), AX.X).then_inc(mx_done["A"].sem, 1)

            @of_batch
            def maxima_cross(bt, k):
                t, c = k // (NPAIR // 2), k % (NPAIR // 2)
                dve.wait_ge(*score["B"].at(bt, k + 1))
                if k == 0:
                    dve.wait_ge(*nm_done["B"].at(bt + -1))
                v.reduce_max(mx["B"][:, t, 4 * c:4 * c + 4],
                             bank(f"Bscore{k}").rearrange("p (a n) -> p a n", a=4)[:, :, 0:LC],
                             AX.X).then_inc(mx_done["B"].sem, 1)

            @of_batch
            def negate(bt, s, t):
                dve.wait_ge(*mx_done[s].at(bt, (t + 1) * MAXES[s] // NT))
                if t == 0:
                    dve.wait_ge(*m_tr[s].at(bt + -1))
                mv_ = mx[s][:, t, :].rearrange("p (a q) -> p q a", q=2)
                v.tensor_scalar(nm[s][:, t, :, 0, :], mv_, -1.0, None, ALU.mult).then_inc(nmhi_done[s].sem, 1)
                dve.wait_ge(*nmhi_done[s].at(bt, t + 1))
                v.scalar_tensor_tensor(out=nm[s][:, t, :, 1, :], in0=mv_, scalar=-1.0,
                                       in1=nm[s][:, t, :, 0, :].bitcast(f32), op0=ALU.mult,
                                       op1=ALU.subtract).then_inc(nm_done[s].sem, 1)

            @of_batch
            def divide(bt, phase, s, t):
                dve.wait_ge(*o_nat[s].at(bt, t + 1))
                src = bank(f"{phase}on{t}").rearrange("p (h w) -> p h w", w=VW)
                if t == 0:
                    dve.wait_ge(*on_use.before(phase, bt))
                v.reciprocal(rden[:, t, :], src[:, :, DH]).then_inc(rden_done[s].sem, 1)
                dve.wait_ge(*rden_done[s].at(bt, t + 1))
                v.tensor_tensor(o_n[:, t, :].rearrange("p (h d) -> p h d", d=DH), src[:, :, 0:DH],
                                rden[:, t, :, None].to_broadcast([P, H, DH]), ALU.mult).then_inc(on_done[s].sem, 1)

            @of_batch
            def output_low(bt, phase, s):
                dve.wait_ge(*ohi_done[s].at(bt))
                dve.wait_ge(*ol_use.before(phase, bt))
                v.tensor_tensor(halves(o_lo), bank(phase + "oT"), halves(o_hi).bitcast(f32), ALU.subtract)\
                    .then_inc(olo_done[s].sem, 1)

            @of_batch
            def residual(bt, phase, s, acc, there):
                dve.wait_ge(*proj_out[s].at(bt))
                dve.wait_ge(*there.at(bt))
                v.tensor_tensor(halves(acc), bank(phase + "out"), halves(acc), ALU.add).then_inc(res_done[s].sem, 1)

            @of_batch
            def gelu_high(bt, k):
                dve.wait_ge(*gelu_done.at(bt, 2 * k + 2))
                if k == 0:
                    dve.wait_ge(*proj_out["C"].at(bt + -1))
                v.tensor_copy(h_hi[:, 2 * k:2 * k + 2, :],
                              h_f[:, k % 2, :].rearrange("p (c n) -> p c n", c=2)).then_inc(hhi_done.sem, 1)

            def body(L_, N, A, B_, T, F):
                statistics(N, "A", x_in, x_loaded)
                variance(N, "A")
                for k in range(A_MAX):
                    maxima_self(A, k)
                    if k == 3:
                        normalise(N, "N", "A", x_in)
                    if k == 5:
                        split_norm(B_, "B")
                    if k == NPAIR - 1:
                        negate(A, "A", 0)
                negate(A, "A", 1)
                rotate_cross_k(B_)
                divide(T, "T", "B", 0)
                divide(T, "T", "B", 1)
                rotate_cross_q(B_, 0)
                output_low(T, "T", "B")
                residual(F, "F", "C", xc, xc_made)
                rotate_cross_q(B_, 1)
                stack_low_cross(B_, 0)
                residual(T, "T", "B", xt, xt_copied)
                stack_low_cross(B_, 1)
                statistics(T, "C", xt, res_done["B"])
                stack_low_cross(B_, 2)
                variance(T, "C")
                split_norm(N, "A")
                normalise(T, "T", "C", xt)
                stack_k_cross(B_, 0)
                stack_k_cross(B_, 1)
                context_low(A)
                for k in range(B_MAX):
                    maxima_cross(B_, k)
                    if k % (NPAIR // 2) == NPAIR // 2 - 1:
                        negate(B_, "B", k // (NPAIR // 2))
                split_norm(T, "C")
                rotate_self(N, 0)
                divide(A, "A", "A", 0)
                divide(A, "A", "A", 1)
                rotate_self(N, 1)
                gelu_high(T, 0)
                stacks_low_self(N, 0)
                output_low(A, "A", "A")
                gelu_high(T, 1)
                stacks_low_self(N, 1)
                residual(A, "A", "A", xa, xa_loaded)
                statistics(A, "B", xa, res_done["A"])
                variance(A, "B")
                gelu_high(T, 2)
                normalise(A, "A", "B", xa)
                gelu_high(T, 3)
            run_turns(dve, [rot_use, rots_use, on_use, ol_use, xn_use, nat_use], body)

        @block.tensor
        def _(pe):
            mm, tr = nc.tensor.matmul, nc.tensor.transpose
            wqkv_, wsa_, wq_, wkv_, wca_, w1_ = (weight(n, NC) for n in ("qkv", "sa", "q", "kv", "ca", "w1"))
            w2_ = weight("w2", NF)
            bank_use = Reuse(HELD, bank_uses)

            def fill(name, bt):
                pe.wait_ge(*bank_use.before(name, bt))
                return bank(name)

            def split_product(out_, terms):
                n = len(terms)
                for k, (l, r) in enumerate(terms):
                    last = mm(out_, l, r, start=(k == 0), stop=(k == n - 1))
                return last

            def three(xh, xl, w, xs, ws):
                wh, wl = w
                return [(x_[:, c, xs], w_[:, c, ws]) for c in range(NC) for x_, w_ in ((xh, wh), (xl, wh), (xh, wl))]

            def by_tiles(o, xh, xl, w, ws):
                for t in range(NT):
                    last = split_product(o[:, t * D:(t + 1) * D], three(xh, xl, w, slice(t * P, (t + 1) * P), ws))
                return last

            @of_batch
            def norm_transpose(bt, phase, s):
                pe.wait_ge(*xn_done[s].at(bt))
                o = fill(phase + "lnT", bt)
                for c in range(NC):
                    for t in range(NT):
                        last = tr(o[:, c * L + t * P:c * L + (t + 1) * P], xn[:, t, c * P:(c + 1) * P], ident[:])
                last.then_inc(ln_t[s].sem, 1)

            @of_batch
            def context_transpose(bt):
                pe.wait_ge(*ctx_loaded.at(bt))
                o = fill("ActxT", bt)
                for c in range(NC):
                    last = tr(o[:, c * LC:(c + 1) * LC], ctx_in[:, c * P:(c + 1) * P], ident[0:LC, 0:LC])
                last.then_inc(ctx_t.sem, 1)

            @of_batch
            def project_qk(bt, t):
                if t == 0:
                    pe.wait_ge(*tlo_done["A"].at(bt))
                o = fill(f"Nqk{t}", bt)
                split_product(o, three(t_hi["A"], t_lo["A"], wqkv_, slice(t * P, (t + 1) * P), slice(0, 2 * D)))\
                    .then_inc(a_proj.sem, 1)

            @of_batch
            def project_v(bt):
                o = fill("Nv", bt)
                by_tiles(o, t_hi["A"], t_lo["A"], wqkv_, slice(2 * D, 3 * D)).then_inc(a_proj.sem, 1)

            @of_batch
            def project_context(bt):
                pe.wait_ge(*ctx_lo.at(bt))
                o = fill("Bkv", bt)
                split_product(o[0:LC, :], three(c_hi, c_lo, wkv_, slice(0, LC), slice(0, 2 * D))).then_inc(b_kv.sem, 1)

            @of_batch
            def project_q(bt):
                pe.wait_ge(*tlo_done["B"].at(bt))
                o = fill("Bq", bt)
                by_tiles(o, t_hi["B"], t_lo["B"], wq_, slice(0, D)).then_inc(b_q.sem, 1)

            def stack_transposes(o, jobs):
                for col, src, rows in jobs:
                    last = tr(o[:, col:col + rows].bitcast(f32r), src, ident_r[0:rows, 0:rows])
                return last

            def pair_of(nat_, t, p, rows=P):
                return nat_[0:rows, t, 2 * p:2 * p + 2, :].rearrange("p h w -> p (h w)")

            @of_batch
            def stacks_self(bt, k):
                if k == 0:
                    pe.wait_ge(*nlo_done["A"].at(bt))
                for name, nat_ in (("Aqst", q_nat), ("Akst", k_nat)):
                    o = fill(f"{name}{k}", bt)
                    stack_transposes(o, [(a * L + t * P, pair_of(nat_, t, 2 * k + a), P)
                                         for a in range(2) for t in range(NT)]).then_inc(st_t["A"].sem, 1)

            @of_batch
            def stacks_cross_q(bt, k):
                if k == 0:
                    pe.wait_ge(*nlo_done["B"].at(bt))
                o = fill(f"Bqst{k}", bt)
                stack_transposes(o, [(a * L + t * P, pair_of(q_nat, t, 2 * k + a), P)
                                     for a in range(2) for t in range(NT)]).then_inc(st_t["B"].sem, 1)

            @of_batch
            def stacks_cross_k(bt, k):
                if k == 0:
                    pe.wait_ge(*nlo_done["B"].at(bt, 1))
                o = fill(f"Bkst{k}", bt)
                stack_transposes(o, [(a * P, pair_of(k_nat, 0, 4 * k + a, LCE), LCE) for a in range(4)])\
                    .then_inc(st_t["B"].sem, 1)

            @of_batch
            def max_transpose(bt, s):
                pe.wait_ge(*nm_done[s].at(bt))
                o = fill(s + "mT", bt)
                for t in range(NT):
                    last = tr(o[0:2 * H, t * P:(t + 1) * P].bitcast(f32r),
                              nm[s][:, t].rearrange("p q j a -> p (q j a)"), ident_r[:])
                last.then_inc(m_tr[s].sem, 1)

            @of_batch
            def scores_self(bt, k):
                t, pair, par = k // NPAIR, 2 * (k % NPAIR // 2), k % 2
                if t == 0 and par == 0:
                    pe.wait_ge(*qst_done["A"].at(bt, k // 2 + 1))
                    pe.wait_ge(*kst_done["A"].at(bt, k // 2 + 1))
                o = fill(f"Ascore{k}", bt)
                r = slice(SROW * par, SROW * par + NS)
                for j in range(2):
                    last = mm(o[:, j * L:(j + 1) * L], q_st["A"][r, pair + j, t * P:(t + 1) * P],
                              k_st_a[r, pair + j, :], start=True, stop=True)
                last.then_inc(score["A"].sem, 1)

            @of_batch
            def scores_cross(bt, k):
                t, c = k // (NPAIR // 2), k % (NPAIR // 2)
                if t == 0:
                    pe.wait_ge(*qst_done["B"].at(bt, k + 1))
                    pe.wait_ge(*kst_done["B"].at(bt, 2 * (k // 2) + 2))
                o = fill(f"Bscore{k}", bt)
                for j in range(2):
                    last = mm(o[:, j * L:(j + 1) * L], q_st["B"][:, 2 * c + j, t * P:(t + 1) * P],
                              k_st_b[:, 2 * c + j].rearrange("p q n -> p (q n)"), start=True, stop=True)
                last.then_inc(score["B"].sem, 1)

            @of_batch
            def shifted_self(bt, h):
                if h == 0:
                    pe.wait_ge(*m_rows["A"].at(bt))
                o, pair = fill(f"Ashift{h}", bt), h // 2
                r = slice(SROW * (h % 2), SROW * (h % 2) + NSM)
                for t in range(NT):
                    last = mm(o[:, t * L:(t + 1) * L], k_st_a[r, pair, t * P:(t + 1) * P], q_st["A"][r, pair, :],
                              start=True, stop=True)
                last.then_inc(shifted["A"].sem, 1)

            @of_batch
            def shifted_cross(bt, pair):
                if pair == 0:
                    pe.wait_ge(*m_rows["B"].at(bt))
                o = fill(f"Tshift{pair}", bt)
                for par in range(2):
                    last = mm(o[0:LC, par * L:(par + 1) * L], k_st_b[:, pair, par, 0:LC], q_st["B"][:, pair, :],
                              start=True, stop=True)
                last.then_inc(shifted["B"].sem, 1)

            @of_batch
            def weighted(bt, phase, s, g_):
                pe.wait_ge(*p_done[s].at(bt, (g_ + 1) * EXPS[s] // NG))
                if g_ == 0:
                    pe.wait_ge(*v_ready[s].at(bt))
                name = f"{phase}pv{g_ // 2}"
                o = (fill(name, bt) if g_ % 2 == 0 else bank(name))[:, (g_ % 2) * L:(g_ % 2 + 1) * L]
                for t in range(NT if s == "A" else 1):
                    for j in range(GRP):
                        h = GRP * g_ + j
                        if s == "A":
                            l, r = v_a[:, t, h, :], probs[:, h % NSLOT, t * L:(t + 1) * L]
                        else:
                            l, r = v_b[:, h, :], probs[0:LC, h // 2, (h % 2) * L:(h % 2 + 1) * L]
                        last = mm(o[VW * j:VW * (j + 1), :], l, r, start=(t == 0),
                                  stop=(s == "B" or t == NT - 1))
                last.then_inc(pv[s].sem, 1)

            @of_batch
            def output_natural(bt, phase, s):
                pe.wait_ge(*o_copied[s].at(bt))
                for t in range(NT):
                    o = fill(f"{phase}on{t}", bt)
                    for g_ in range(NG):
                        last = tr(o[:, g_ * P:(g_ + 1) * P],
                                  o_st[:, g_ // 2, (g_ % 2) * L + t * P:(g_ % 2) * L + (t + 1) * P], ident[:])
                    last.then_inc(o_nat[s].sem, 1)

            @of_batch
            def output_transpose(bt, phase, s):
                pe.wait_ge(*on_done[s].at(bt))
                o = fill(phase + "oT", bt)
                for c in range(NC):
                    for t in range(NT):
                        last = tr(o[:, c * L + t * P:c * L + (t + 1) * P], o_n[:, t, c * P:(c + 1) * P], ident[:])
                last.then_inc(o_tr[s].sem, 1)

            @of_batch
            def output_product(bt, phase, s):
                pe.wait_ge(*olo_done[s].at(bt))
                o = fill(phase + "out", bt)
                by_tiles(o, o_hi, o_lo, wsa_ if s == "A" else wca_, slice(0, D)).then_inc(proj_out[s].sem, 1)

            @of_batch
            def hidden(bt, k):
                if k == 0:
                    pe.wait_ge(*tlo_done["C"].at(bt))
                o = fill(f"Tf{k}", bt)
                for j in range(2):
                    f = slice((2 * k + j) * P, (2 * k + j + 1) * P)
                    last = split_product(o[:, j * L:(j + 1) * L],
                                         [(w_[:, c, f], x_[:, c, :]) for c in range(NC)
                                          for w_, x_ in ((w1_[0], t_hi["C"]), (w1_[0], t_lo["C"]),
                                                         (w1_[1], t_hi["C"]))])
                last.then_inc(f1.sem, 1)

            @of_batch
            def feed_forward_out(bt, part):
                o = fill("Fout", bt) if part == 0 else bank("Fout")
                per_tile = A_MAX // NT
                t, f = part // per_tile, part % per_tile
                if t == 0 and f % 2 == 0:
                    pe.wait_ge(*hlo_done.at(bt, f // 2 + 1))
                for n, (h_, w_) in enumerate(((h_hi, w2_[0]), (h_lo, w2_[0]), (h_hi, w2_[1]))):
                    last = mm(o[:, t * D:(t + 1) * D], h_[:, f, t * P:(t + 1) * P], w_[:, f, :],
                              start=(f == 0 and n == 0), stop=(f == NF - 1 and n == 2))
                if part == A_MAX - 1:
                    last.then_inc(proj_out["C"].sem, 1)

            pe.wait_ge(ld_const, 8 * 16)
            for m in range(12):
                w = (rot_c, o_st, h_f)[m // 4][:].rearrange("p a b -> p (a b)").rearrange("p (c n) -> p c n", c=NC)
                for c in range(NC):
                    last = mm(psum["gen", 0][:, m * B:(m + 1) * B], w[:, c, (m % 4) * P:(m % 4 + 1) * P],
                              cond_s[:, c, :], start=(c == 0), stop=(c == NC - 1))
            last.then_inc(gb_product, 1)
            pe.wait_ge(gb_ready, 12)
            pe.wait_ge(const_ready, 5)
            pe.wait_ge(w_lo_ready, len(names))

            def body(L_, N, A, B_, T, F):
                stacks_self(A, 0)
                feed_forward_out(F, 0)
                stacks_self(A, 1)
                for k in range(A_MAX):
                    scores_self(A, k)
                    if k < 11:
                        feed_forward_out(F, k + 1)
                    if k == 1:
                        stacks_self(A, 2)
                        norm_transpose(B_, "B", "B")
                    if k == 3:
                        stacks_self(A, 3)
                    if 5 <= k < 5 + B_EXP:
                        shifted_cross(T, k - 5)
                    if k == 9:
                        norm_transpose(N, "N", "A")
                    if k >= 8 and k % 2 == 0:
                        weighted(T, "T", "B", (k - 8) // 2)
                    if k == 13:
                        project_context(B_)
                feed_forward_out(F, 12)
                feed_forward_out(F, 13)
                max_transpose(A, "A")
                output_natural(T, "T", "B")
                project_q(B_)
                output_transpose(T, "T", "B")
                feed_forward_out(F, 14)
                feed_forward_out(F, 15)
                for h in range(A_EXP):
                    shifted_self(A, h)
                    if h == 1:
                        output_product(T, "T", "B")
                    if h % GRP == 1 and h > GRP:
                        weighted(A, "A", "A", h // GRP - 1)
                    if h == 4:
                        stacks_cross_k(B_, 0)
                        stacks_cross_k(B_, 1)
                    if 5 <= h < 9:
                        stacks_cross_q(B_, h - 5)
                    if h == 7:
                        context_transpose(A)
                    if 9 <= h < 13:
                        scores_cross(B_, 2 * (h - 9))
                        scores_cross(B_, 2 * (h - 9) + 1)
                    if h == 10:
                        norm_transpose(T, "T", "C")
                    if h == 13:
                        project_qk(N, 0)
                    if h == 15:
                        project_qk(N, 1)
                weighted(A, "A", "A", NG - 1)
                max_transpose(B_, "B")
                hidden(T, 0)
                output_natural(A, "A", "A")
                hidden(T, 1)
                output_transpose(A, "A", "A")
                project_v(N)
                hidden(T, 2)
                output_product(A, "A", "A")
                hidden(T, 3)
            run_turns(pe, [bank_use], body)


_OUT = ((B, L, D), "float32")


def kernel(**inputs):
    import numpy as np
    import concourse.bacc as bacc
    from concourse.bass_utils import run_bass_kernel_spmd

    f = {k: np.asarray(v) for k, v in inputs.items()}
    w = {k[len("L0_xcond_"):]: v for k, v in f.items() if k.startswith("L0_xcond_")}
    half = DH // 2
    inv_freq = (np.float32(1.0) / np.float32(10000.0) ** (np.arange(half, dtype=np.float32) / np.float32(half)))
    ang = np.arange(L, dtype=np.float32)[:, None] * inv_freq.astype(np.float32)[None, :]
    rope = np.concatenate([np.cos(ang), np.sin(ang), -np.sin(ang)], axis=1).astype(np.float32)
    arrays = {
        "x": f["x"], "ctx": f["ctx_1024"], "cond_t": f["cond_1024"].T, "rope": rope,
        "wqkv": w["qkv_w"].T, "wsa": w["sa_out_w"].T, "wq": w["q_w"].T,
        "wkv": np.concatenate([w["k_w"].T, w["v_w"].T], axis=1), "wca": w["ca_out_w"].T,
        "w1": w["ffn_w1"].T, "w2": w["ffn_w2"].T,
        "lnw": np.stack([w[f"ln{k}_w"].T for k in (1, 2, 3)]),
        "lnb": np.concatenate([w[f"ln{k}_b"].reshape(4, P).T for k in (1, 2, 3)], axis=1),
        "b1": w["ffn_b1"].reshape(NF, P).T, "b2": w["ffn_b2"],
    }
    nc = bacc.Bacc("TRN2", target_bir_lowering=False, num_devices=1)
    host, args = {}, []
    for name, a in arrays.items():
        a = np.ascontiguousarray(a)
        host[f"in_{name}"] = a
        args.append(nc.dram_tensor(f"in_{name}", a.shape, mybir.dt.from_np(a.dtype), kind="ExternalInput").ap())
    args.append(nc.dram_tensor("out_x", _OUT[0], mybir.dt.float32, kind="ExternalOutput").ap())
    layer_kernel(nc, *args)
    r = run_bass_kernel_spmd(nc, [host], core_ids=[0])
    return r.results[0]["out_x"]
```

```python
from contextlib import ExitStack

import concourse.bass as bass
from concourse import mybir

B, L, D, H, DH, DFF, LC = 32, 256, 256, 16, 16, 1024, 77
P = 128
NT = L // P
NC = D // P
NF = DFF // P
NPAIR = H // 2
SROW = P // 2
NS = 3 * DH
NSM = NS + 2
VW = 32
GRP = P // VW
NG = H // GRP
LCE = LC + LC % 2
EPS = 1e-5
SCALE = 1.0 / DH ** 0.5
A_STACKS = NPAIR
B_STACKS = NPAIR // 2 + 2
A_MAX, B_MAX = NT * NPAIR, NT * NPAIR // 2
A_EXP, B_EXP = H, H // 2
NSLOT = 8
PHASE = {"L": 2, "N": 1, "A": 0, "B": -1, "T": -2, "F": -3}
FIRST_LOOP, END_LOOP = 4, B - 2


class Batch:

    def __init__(self, reg, off):
        self.reg, self.off = reg, off

    def __add__(self, n):
        return Batch(self.reg, self.off + n)

    def times(self, per, k=0):
        c = self.off * per + k
        if self.reg is None:
            return c
        v = self.reg * per if per != 1 else self.reg
        return v + c if c else v


class Event:

    def __init__(self, sem, per, inc, held):
        self.sem, self.per, self.inc, self.held = sem, per, inc, held

    def at(self, batch, k=None):
        if batch.reg is None and batch.off > B - 1:
            batch, k = Batch(None, B - 1), None
        v = batch.times(self.per * self.inc, self.inc * (self.per if k is None else k))
        return self.held if isinstance(v, int) and v <= 0 else (self.sem, v)


class Reuse:

    def __init__(self, held, uses):
        self.held = held
        self.uses = {u[0]: u for u in uses}
        self.last_of_turn = {u[1]: u for u in uses}
        self.last = {}

    def before(self, name, batch):
        _, slot, _, _ = use = self.uses[name]
        end = self.held
        if slot in self.last:
            (_, _, event, k), before = self.last[slot]
            end = event.at(before, k)
        self.last[slot] = (use, batch)
        return end

    def turn_before(self, turn):
        self.last = {s: (u, turn + (PHASE[u[0][0]] - 1)) for s, u in self.last_of_turn.items()}


def of_batch(step):
    def run(batch, *args):
        if batch is not None:
            step(batch, *args)
    return run


def run_turns(eng, reuses, body, setup=None, first=-2):
    def peeled(t):
        body(*(Batch(None, t + off) if 0 <= t + off < B else None for off in PHASE.values()))
    for t in range(first, FIRST_LOOP):
        if setup and t in setup:
            setup[t]()
        peeled(t)
    with eng.Fori(FIRST_LOOP, END_LOOP) as i:
        for r in reuses:
            r.turn_before(Batch(i, 0))
        body(*(Batch(i, off) for off in PHASE.values()))
    for r in reuses:
        r.turn_before(Batch(None, END_LOOP))
    for t in range(END_LOOP, B + 3):
        peeled(t)


def layer_kernel(nc, x, ctx, cond_t, rope, wqkv, wsa, wq, wkv, wca, w1, w2, lnw, lnb, b1, b2, out):
    f32, f32r = mybir.dt.float32, mybir.dt.float32r
    ALU, ACT, AX = mybir.AluOpType, mybir.ActivationFunctionType, mybir.AxisListType
    x_d = x.rearrange("b (t p) d -> b p t d", p=P)
    out_d = out.rearrange("b (t p) d -> b p t d", p=P)

    with ExitStack() as es:
        def sb(name, shape, dt=f32):
            return es.enter_context(nc.sbuf_tensor(name, shape, dt))

        def sem(name):
            return es.enter_context(nc.semaphore(name))

        def event(name, per, inc=1):
            return Event(sem(name), per, inc, HELD)

        sources = [("qkv", NC * 3 * D, wqkv), ("sa", NC * D, wsa), ("q", NC * D, wq), ("kv", NC * 2 * D, wkv),
                   ("w1", NC * DFF, w1), ("w2", NF * D, w2), ("ca", NC * D, wca)]
        names, total = {}, 0
        for n, cols, src in sources:
            names[n] = (total, cols, src)
            total += cols
        w_hi, w_lo = sb("w_hi", [P, total], f32r), sb("w_lo", [P, total], f32r)

        def weight(name, chunks):
            a, cols, _ = names[name]
            return (w_hi[:, a:a + cols].rearrange("p (c n) -> p c n", c=chunks),
                    w_lo[:, a:a + cols].rearrange("p (c n) -> p c n", c=chunks))

        ident, ident_r = sb("ident", [P, P]), sb("ident_r", [P, P], f32r)
        rope_t = sb("rope_t", [P, NT, 3, 8])
        gb = sb("gb", [P, 3, 4, B])
        lnb_t = sb("lnb_t", [P, 12])
        b1_t, b2_t = sb("b1_t", [P, NF]), sb("b2_t", [P, D])
        minus_half = sb("minus_half", [P, NT])
        fence = {s: sb(f"fence_{s}", [P, 1]) for s in "ABC"}
        act_fence = sb("act_fence", [P, 1])
        pool_fence = sb("pool_fence", [P, 1])
        cond_s = sb("cond_s", [P, NC, B])
        x_in, xa, xt, xc = (sb(n, [P, NT, D]) for n in ("x_in", "xa", "xt", "xc"))
        ctx_in = sb("ctx_in", [LC, D])
        xn = {"A": sb("xn_A", [P, NT, D]), "B": sb("xn_BC", [P, NT, D])}
        xn["C"] = xn["B"]
        stats = {s: sb(f"stats_{s}", [P, NT, 6]) for s in "ABC"}
        mv = {s: sb(f"mv_{s}", [P, NT, 2]) for s in "ABC"}
        ve = {s: sb(f"ve_{s}", [P, NT]) for s in "ABC"}
        rstd = {s: sb(f"rstd_{s}", [P, NT]) for s in "ABC"}
        t_f = sb("t_f", [P, NC, L])
        t_hi = {s: sb(f"t_hi_{s}", [P, NC, L], f32r) for s in "ABC"}
        t_lo = {s: sb(f"t_lo_{s}", [P, NC, L], f32r) for s in "ABC"}
        c_hi, c_lo = sb("c_hi", [P, NC, LC], f32r), sb("c_lo", [P, NC, LC], f32r)
        rot_c = sb("rot_c", [P, NT, 2 * D])
        rot_s = sb("rot_s", [P, 2 * D])
        rk_c, rk_s = sb("rk_c", [LC, D]), sb("rk_s", [LC, D])
        q_nat = sb("q_nat", [P, NT, H, SROW], f32r)
        k_nat = sb("k_nat", [P, NT, H, SROW], f32r)
        q_st = {s: sb(f"q_st_{s}", [P, NPAIR, L], f32r) for s in "AB"}
        k_st_a = sb("k_st_a", [P, NPAIR, L], f32r)
        k_st_b = sb("k_st_b", [P, NPAIR, 2, P], f32r)
        v_a = sb("v_a", [P, NT, H, VW])
        v_b = sb("v_b", [LC, H, VW])
        mx = {s: sb(f"mx_{s}", [P, NT, H]) for s in "AB"}
        nm = {s: sb(f"nm_{s}", [P, NT, 2, 2, NPAIR], f32r) for s in "AB"}
        m_rows_t = sb("m_rows_t", [4 * H, L], f32r)
        m_t = {"A": m_rows_t[0:2 * H, :], "B": m_rows_t[2 * H:4 * H, :]}
        probs = sb("probs", [P, NSLOT, 2 * L])
        o_st = sb("o_st", [P, 2, 2 * L])
        rden = sb("rden", [P, NT, H])
        o_n = sb("o_n", [P, NT, D])
        o_hi, o_lo = sb("o_hi", [P, NC, L], f32r), sb("o_lo", [P, NC, L], f32r)
        h_f = sb("h_f", [P, 2, 2 * L])
        h_hi, h_lo = sb("h_hi", [P, NF, L], f32r), sb("h_lo", [P, NF, L], f32r)

        psum = {}
        for name in ("gen", "maxs", "exps", "pvs"):
            pair = es.enter_context(nc.psum_tensor(name, [P, 2 * 512], f32))
            psum[name, 0], psum[name, 1] = pair[:, 0:512], pair[:, 512:1024]

        ld_first, ld_qkv, ld_norms, ld_w1, ld_rest = (sem(f"ld_{n}") for n in ("first", "qkv", "norms", "w1", "rest"))
        w_hi_ready, w_lo_ready, w2_lo_ready = sem("w_hi_ready"), sem("w_lo_ready"), sem("w2_lo_ready")
        pool_zeroed, const_ready = sem("pool_zeroed"), sem("const_ready")
        gb_product, gb_ready = sem("gb_product"), sem("gb_ready")
        HELD = (w_hi_ready, 1)

        x_loaded, ctx_loaded, out_stored = (event(n, 1, 16) for n in ("x_loaded", "ctx_loaded", "out_stored"))
        xa_loaded, xt_copied, xc_made = event("xa_loaded", 1, 16), event("xt_copied", 1), event("xc_made", 1)

        def per_layer(what, layers, per, inc=1):
            return {s: event(f"{s}_{what}", per[s] if isinstance(per, dict) else per, inc) for s in layers}

        stat_done, mv_done, var_done = (per_layer(n, "ABC", k) for n, k in (("stat", NT), ("mv", NT), ("var", 1)))
        rstd_done, xn_done, ln_t = (per_layer(n, "ABC", k) for n, k in (("rstd", 1), ("xn", NT), ("lnT", 1)))
        t_done, thi_done, tlo_done = (per_layer(n, "ABC", k) for n, k in (("t", NC), ("thi", 1), ("tlo", 1)))
        ctx_t, ctx_hi, ctx_lo = event("ctx_t", 1), event("ctx_hi", 1), event("ctx_lo", 1)
        a_proj, b_kv, b_q = event("a_proj", NT + 1), event("b_kv", 1), event("b_q", 1)
        v_ready = per_layer("v", "AB", 1)
        TILES = {"A": NT, "B": NT + 1}
        cos_done, sin_done = (per_layer(n, "AB", TILES) for n in ("cos", "sin"))
        rot_done = per_layer("rot", "AB", {s: 2 * n for s, n in TILES.items()})
        PIECES = {"A": 2 * NT, "B": NT + 1}
        nhi_done = per_layer("nhi", "AB", PIECES)
        nlo_done = per_layer("nlo", "AB", PIECES)
        STACKS, MAXES, EXPS = ({"A": a, "B": b} for a, b in ((A_STACKS, B_STACKS), (A_MAX, B_MAX), (A_EXP, B_EXP)))
        st_t = per_layer("stT", "AB", STACKS)
        qst_done = per_layer("qst", "AB", NPAIR // 2)
        kst_done = per_layer("kst", "AB", NPAIR // 2)
        score, mx_done = per_layer("score", "AB", MAXES), per_layer("mx", "AB", MAXES)
        nmhi_done, nm_done = per_layer("nmhi", "AB", NT), per_layer("nm", "AB", NT)
        m_tr, m_copied, m_rows = (per_layer(n, "AB", 1) for n in ("mT", "mcopy", "mrows"))
        m_rows = {s: Event(e.sem, 2, 16, HELD) for s, e in m_rows.items()}
        shifted, p_done = per_layer("shifted", "AB", EXPS), per_layer("p", "AB", EXPS)
        pv, o_copied = per_layer("pv", "AB", NG), per_layer("ocopy", "AB", 2)
        o_nat, rden_done, on_done = (per_layer(n, "AB", NT) for n in ("onat", "rden", "on"))
        o_tr, ohi_done, olo_done = (per_layer(n, "AB", 1) for n in ("oT", "ohi", "olo"))
        proj_out = per_layer("proj", "ABC", 1)
        res_done = per_layer("res", "ABC", 1)
        table_loaded = event("table_loaded", 2)
        f1, gelu_done = event("f1", NF // 2), event("gelu", NF)
        hhi_done, hlo_done = event("hhi", NF // 2), event("hlo", NF // 2)

        bank_uses = [("Fout", ("gen", 0), res_done["C"], 1),
                     ("BlnT", ("gen", 1), t_done["B"], NC),
                     ("NlnT", ("gen", 1), t_done["A"], NC),
                     ("Bkv", ("gen", 1), v_ready["B"], 1)]
        stack_banks = [(("exps", 0), ("exps", 1), ("pvs", 0))[k % 3] for k in range(A_STACKS)]
        for k in range(NPAIR // 2):
            bank_uses += [(f"Aqst{k}", stack_banks[2 * k], qst_done["A"], k + 1),
                          (f"Akst{k}", stack_banks[2 * k + 1], kst_done["A"], k + 1)]
        score_banks = [(("maxs", 0), ("maxs", 1), ("pvs", 1))[k % 3] if k < 9 else ("maxs", (k - 9) % 2)
                       for k in range(A_MAX)]
        bank_uses += [(f"Ascore{k}", score_banks[k], mx_done["A"], k + 1) for k in range(A_MAX)]
        bank_uses += [(f"Tshift{k}", ("exps", k % 2), p_done["B"], k + 1) for k in range(B_EXP)]
        bank_uses += [(f"Tpv{k}", ("pvs", k), o_copied["B"], k + 1) for k in range(2)]
        bank_uses += [("AmT", ("maxs", 0), m_copied["A"], 1),
                      ("Ton0", ("exps", 0), on_done["B"], 1), ("Ton1", ("exps", 1), on_done["B"], 2),
                      ("Bq", ("pvs", 0), sin_done["B"], NT + 1),
                      ("ToT", ("maxs", 1), olo_done["B"], 1),
                      ("Tout", ("maxs", 0), res_done["B"], 1)]
        shift_banks = [(("exps", 0), ("exps", 1), ("maxs", 1))[k % 3] if k < 9 else ("exps", (k - 9) % 2)
                       for k in range(A_EXP)]
        bank_uses += [(f"Ashift{k}", shift_banks[k], p_done["A"], k + 1) for k in range(A_EXP)]
        bank_uses += [("Apv0", ("pvs", 0), o_copied["A"], 1)]
        bank_uses += [("Nqk0", ("gen", 1), sin_done["A"], 1)]
        b_stack_banks = (("gen", 0), ("pvs", 1))
        bank_uses += [(f"Bkst{k}", b_stack_banks[k % 2], kst_done["B"], 2 * k + 2) for k in range(2)]
        bank_uses += [(f"Bqst{k}", b_stack_banks[k % 2], qst_done["B"], k + 1) for k in range(NPAIR // 2)]
        bank_uses += [(f"Bscore{k}", ("maxs", k % 2), mx_done["B"], k + 1) for k in range(B_MAX)]
        bank_uses += [("Apv1", ("pvs", 1), o_copied["A"], 2),
                      ("TlnT", ("gen", 0), t_done["C"], NC),
                      ("Nqk1", ("gen", 0), sin_done["A"], 2),
                      ("BmT", ("maxs", 0), m_copied["B"], 1)]
        bank_uses += [(f"Tf{k}", ("maxs", 1 - k % 2), gelu_done, 2 * k + 2) for k in range(NF // 2)]
        bank_uses += [("Aon0", ("exps", 0), on_done["A"], 1), ("Aon1", ("exps", 1), on_done["A"], 2),
                      ("AoT", ("exps", 0), olo_done["A"], 1),
                      ("Aout", ("exps", 1), res_done["A"], 1),
                      ("Nv", ("gen", 1), v_ready["A"], 1),
                      ("ActxT", ("gen", 0), ctx_lo, 1)]
        bank_of = {name: where for name, where, _, _ in bank_uses}

        def bank(name):
            return psum[bank_of[name]]

        def halves(t):
            return t[:].rearrange("p c n -> p (c n)")

        flat_probs = probs[:].rearrange("p a b -> p (a b)")
        after_qkv = names["qkv"][1]
        stage = {"qkv": flat_probs[:, 0:after_qkv], "w1": flat_probs[:, after_qkv:after_qkv + names["w1"][1]],
                 "q": flat_probs[:, 0:names["q"][1]], "kv": flat_probs[:, names["q"][1]:after_qkv],
                 "w2": flat_probs[:, after_qkv:after_qkv + names["w2"][1]], "sa": halves(xt), "ca": halves(o_n)}

        def lnw_stage(k):
            return (rot_c, o_st, h_f)[k][:].rearrange("p a b -> p (a b)").rearrange("p (c n) -> p c n", c=NC)

        def columns(name):
            a, cols, _ = names[name]
            return slice(a, a + cols)

        gb_bank = psum["pvs", 1]

        block = es.enter_context(nc.Block())

        @block.sync
        def _(sp):
            def load(dst, src, signal):
                sp.dma_start(dst, src).then_inc(signal, 16)

            def load_weight(name, signal):
                _, cols, src = names[name]
                load(stage[name].rearrange("p (c n) -> p c n", c=src.shape[0] // P),
                     src.rearrange("(c p) n -> p c n", p=P), signal)

            def load_norm_weight(k, signal):
                load(lnw_stage(k), lnw[k].rearrange("(c p) n -> p c n", p=P), signal)

            load(cond_s[:], cond_t.rearrange("(c p) b -> p c b", p=P), ld_first)
            load_norm_weight(0, ld_first)
            load(lnb_t[:], lnb, ld_first)
            load(rope_t[:].rearrange("p t k d -> p t (k d)"), rope.rearrange("(t p) n -> p t n", p=P), ld_first)
            load_weight("qkv", ld_qkv)
            load(x_in[:], x_d[0], x_loaded.sem)
            load_norm_weight(1, ld_norms)
            load_norm_weight(2, ld_norms)
            load(b1_t[:], b1, ld_rest)
            load(b2_t[:], b2[None, :].to_broadcast([P, D]), ld_rest)
            load_weight("sa", ld_rest)
            load_weight("ca", ld_rest)
            load_weight("w1", ld_w1)
            sp.wait_ge(w_lo_ready, 1)
            load_weight("q", ld_rest)
            load_weight("kv", ld_rest)
            sp.wait_ge(w_lo_ready, 2)
            load_weight("w2", ld_rest)

            @of_batch
            def max_rows(bt, s):
                sp.wait_ge(*m_copied[s].at(bt))
                for par in range(2):
                    row, r0 = SROW * par + NS, 2 * par * NPAIR
                    sp.dma_start(q_st[s][row:row + 2, :, :].bitcast(f32),
                                 m_t[s][r0:r0 + 2 * NPAIR, :].bitcast(f32)).then_inc(m_rows[s].sem, 16)

            @of_batch
            def load_input(bt):
                sp.wait_ge(*xn_done["A"].at(bt + -1))
                sp.dma_start(x_in[:], x_d[bt.times(1)]).then_inc(x_loaded.sem, 16)

            @of_batch
            def store(bt):
                sp.wait_ge(*res_done["C"].at(bt))
                sp.dma_start(out_d[bt.times(1)], xc[:]).then_inc(out_stored.sem, 16)

            @of_batch
            def load_batch(bt):
                sp.wait_ge(*ctx_t.at(bt + -1))
                sp.dma_start(ctx_in[:], ctx[bt.times(1)]).then_inc(ctx_loaded.sem, 16)
                sp.wait_ge(*xt_copied.at(bt + -1))
                sp.dma_start(xa[:], x_d[bt.times(1)]).then_inc(xa_loaded.sem, 16)

            def body(L_, N, A, B_, T, F):
                load_input(L_)
                max_rows(A, "A")
                store(F)
                load_batch(A)
                max_rows(B_, "B")
            run_turns(sp, [], body, first=-1)
            sp.wait_ge(out_stored.sem, 16 * B)

        @block.gpsimd
        def _(pool):
            g = nc.gpsimd
            v_a_ht = v_a[:].rearrange("p t h w -> p (t h) w")
            k_nat_ht = k_nat[:].rearrange("p t h w -> p (t h) w")
            g.memset(ident[:], 0.0).then_inc(pool_zeroed, 1)
            g.memset(minus_half[:], -0.5).then_inc(const_ready, 1)
            g.memset(v_a_ht[:, :, DH:VW], 0.0).then_inc(pool_zeroed, 1)
            g.memset(v_b[:, :, DH:VW], 0.0).then_inc(pool_zeroed, 1)
            g.memset(q_nat[:].bitcast(f32), 0.0).then_inc(pool_zeroed, 1)
            g.memset(k_nat[:].bitcast(f32), 0.0).then_inc(pool_zeroed, 1)
            g.memset(k_st_b[:].bitcast(f32), 0.0).then_inc(pool_zeroed, 1)
            pool.wait_ge(pool_zeroed, 6)
            g.affine_select(out=ident[:], in_=ident[:], compare_op=ALU.not_equal, fill=1.0, base=0,
                            pattern=[[-1, P]], channel_multiplier=1).then_inc(pool_zeroed, 1)
            g.memset(v_a_ht[:, :, DH:DH + 1], 1.0).then_inc(const_ready, 1)
            g.memset(v_b[:, :, DH:DH + 1], 1.0).then_inc(const_ready, 1)
            g.memset(k_nat_ht[:, :, NS:NSM].bitcast(f32), 1.0).then_inc(const_ready, 1)
            pool.wait_ge(pool_zeroed, 7)
            g.tensor_copy(ident_r[:], ident[:]).then_inc(const_ready, 1)
            def finish_setup():
                pool.wait_ge(w_hi_ready, 3)
                g.tensor_tensor(w_lo[:, columns("w2")], stage["w2"], w_hi[:, columns("w2")].bitcast(f32),
                                ALU.subtract).then_inc(w2_lo_ready, 1)

            @of_batch
            def power(bt, s):
                pool.wait_ge(*var_done[s].at(bt))
                pool.wait_ge(*xn_done[s].at(bt + -1))
                g.tensor_tensor(rstd[s][:], ve[s][:], minus_half[:], ALU.pow).then_inc(rstd_done[s].sem, 1)

            @of_batch
            def residual_and_bias(bt):
                pool.wait_ge(*xn_done["C"].at(bt))
                pool.wait_ge(*out_stored.at(bt + -1))
                g.tensor_tensor(xc[:], xt[:], b2_t[:, None, :].to_broadcast([P, NT, D]), ALU.add)\
                    .then_inc(xc_made.sem, 1)

            @of_batch
            def move_residual(bt):
                pool.wait_ge(*xn_done["B"].at(bt))
                pool.wait_ge(*xc_made.at(bt + -1))
                g.tensor_tensor(pool_fence[:, 0:1], minus_half[:, 0:1], minus_half[:, 0:1], ALU.mult)
                g.tensor_copy(xt[:], xa[:]).then_inc(xt_copied.sem, 1)

            @of_batch
            def gelu_low(bt, k):
                pool.wait_ge(*hhi_done.at(bt, k + 1))
                if k == 0:
                    pool.wait_ge(*proj_out["C"].at(bt + -1))
                g.tensor_tensor(h_lo[:, 2 * k:2 * k + 2, :], h_f[:, k % 2, :].rearrange("p (c n) -> p c n", c=2),
                                h_hi[:, 2 * k:2 * k + 2, :].bitcast(f32), ALU.subtract).then_inc(hlo_done.sem, 1)

            def body(L_, N, A, B_, T, F):
                power(T, "C")
                power(L_, "A")
                residual_and_bias(T)
                move_residual(B_)
                gelu_low(T, 0)
                gelu_low(T, 1)
                power(A, "B")
                gelu_low(T, 2)
                gelu_low(T, 3)
            run_turns(pool, [], body, {0: finish_setup})

        @block.scalar
        def _(act):
            s_ = nc.scalar
            t_use = Reuse(HELD, [("B", 0, tlo_done["B"], 1), ("N", 0, tlo_done["A"], 1), ("T", 0, tlo_done["C"], 1)])
            p_use = Reuse(HELD, [(f"T{k}", k, pv["B"], k // 2 + 1) for k in range(B_EXP)]
                          + [(f"A{h}", h % NSLOT, pv["A"], h // GRP + 1) for h in range(A_EXP)])
            o_use = Reuse(HELD, [(f"T{k}", k, o_nat["B"], NT) for k in range(2)]
                          + [(f"A{k}", k, o_nat["A"], NT) for k in range(2)])
            oh_use = Reuse(HELD, [("T", 0, proj_out["B"], 1), ("A", 0, proj_out["A"], 1)])
            nat_use = Reuse(HELD, [("B", 0, st_t["B"], B_STACKS), ("N", 0, st_t["A"], A_STACKS)])
            h_use = Reuse(HELD, [(f"T{k}", k % 2, hlo_done, k + 1) for k in range(NF // 2)])

            def column(ln, c, bt):
                return gb[:, ln, c, bt.off:bt.off + 1] if bt.reg is None else gb[:, ln, c, bass.ds(bt.times(1), 1)]

            @of_batch
            def load_table(bt, k, function):
                act.wait_ge(*table_loaded.at(bt, k))
                s_.activation(act_fence[:], minus_half[:, 0:1], function).then_inc(table_loaded.sem, 1)

            @of_batch
            def modulate(bt, phase, s):
                ln = "ABC".index(s)
                act.wait_ge(*ln_t[s].at(bt))
                act.wait_ge(*t_use.before(phase, bt))
                for c in range(NC):
                    s_.activation(t_f[:, c, :], bank(phase + "lnT")[:, c * L:(c + 1) * L], ACT.Identity,
                                  scale=column(ln, c, bt), bias=column(ln, NC + c, bt)).then_inc(t_done[s].sem, 1)

            @of_batch
            def context_high(bt):
                act.wait_ge(*ctx_t.at(bt))
                act.wait_ge(*b_kv.at(bt + -1))
                s_.activation(halves(c_hi), bank("ActxT")[:, 0:NC * LC], ACT.Copy).then_inc(ctx_hi.sem, 1)

            @of_batch
            def values_self(bt):
                act.wait_ge(*a_proj.at(bt, NT + 1))
                act.wait_ge(*pv["A"].at(bt + -1))
                s_.activation(v_a[:].rearrange("p t h w -> p (t h) w")[:, :, 0:DH],
                              bank("Nv").rearrange("p (a d) -> p a d", d=DH), ACT.Copy).then_inc(v_ready["A"].sem, 1)

            @of_batch
            def values_cross(bt):
                act.wait_ge(*b_kv.at(bt))
                act.wait_ge(*sin_done["B"].at(bt, 1))
                act.wait_ge(*pv["B"].at(bt + -1))
                s_.activation(v_b[:, :, 0:DH], bank("Bkv")[0:LC, D:2 * D].rearrange("p (h d) -> p h d", d=DH),
                              ACT.Copy).then_inc(v_ready["B"].sem, 1)

            def stack_high(s, src, dst, blocks):
                out_ = dst[:, :, 0:NS].rearrange("p h (b d) -> p h b d", d=DH)[:, :, blocks, :]
                s_.activation(out_, src.rearrange("p (h d) -> p h d", d=DH)[:, :, None, :]
                              .to_broadcast([out_.shape[0], H, 2, DH]), ACT.Copy).then_inc(nhi_done[s].sem, 1)

            @of_batch
            def stacks_high_self(bt, t):
                act.wait_ge(*rot_done["A"].at(bt, 2 * t + 2))
                if t == 0:
                    act.wait_ge(*nat_use.before("N", bt))
                stack_high("A", rot_c[:, t, 0:D], q_nat[:, t], slice(0, 3, 2))
                stack_high("A", rot_c[:, t, D:2 * D], k_nat[:, t], slice(0, 2))

            @of_batch
            def stack_high_cross(bt, k):
                act.wait_ge(*rot_done["B"].at(bt, 2 * k + 2))
                if k == 0:
                    act.wait_ge(*nat_use.before("B", bt))
                    stack_high("B", rk_c[:, :], k_nat[0:LC, 0], slice(0, 2))
                else:
                    stack_high("B", rot_c[:, k - 1, 0:D], q_nat[:, k - 1], slice(0, 3, 2))

            @of_batch
            def stacks_self(bt, k):
                act.wait_ge(*st_t["A"].at(bt, 2 * k + 1))
                if k == 0:
                    act.wait_ge(*shifted["A"].at(bt + -1))
                s_.activation(q_st["A"][:, 2 * k:2 * k + 2, :], bank(f"Aqst{k}").rearrange("p (a n) -> p a n", a=2),
                              ACT.Copy).then_inc(qst_done["A"].sem, 1)
                act.wait_ge(*st_t["A"].at(bt, 2 * k + 2))
                s_.activation(k_st_a[:, 2 * k:2 * k + 2, :], bank(f"Akst{k}").rearrange("p (a n) -> p a n", a=2),
                              ACT.Copy).then_inc(kst_done["A"].sem, 1)

            @of_batch
            def stack_q_cross(bt, k):
                act.wait_ge(*st_t["B"].at(bt, 2 + k + 1))
                if k == 0:
                    act.wait_ge(*shifted["B"].at(bt + -1))
                s_.activation(q_st["B"][:, 2 * k:2 * k + 2, :], bank(f"Bqst{k}").rearrange("p (a n) -> p a n", a=2),
                              ACT.Copy).then_inc(qst_done["B"].sem, 1)

            @of_batch
            def max_rows(bt, s):
                act.wait_ge(*m_tr[s].at(bt))
                act.wait_ge(*m_rows[s].at(bt + -1))
                s_.activation(m_t[s], bank(s + "mT")[0:2 * H, 0:L], ACT.Copy).then_inc(m_copied[s].sem, 1)

            @of_batch
            def exps(bt, phase, s, k, rows):
                act.wait_ge(*shifted[s].at(bt, k + 1))
                act.wait_ge(*p_use.before(f"{phase}{k}", bt))
                s_.activation(probs[0:rows, k % NSLOT, :], bank(f"{phase}shift{k}")[0:rows, :], ACT.Exp,
                              scale=SCALE).then_inc(p_done[s].sem, 1)

            @of_batch
            def outputs(bt, phase, s, k):
                act.wait_ge(*pv[s].at(bt, 2 * k + 2))
                act.wait_ge(*o_use.before(f"{phase}{k}", bt))
                s_.activation(o_st[:, k, :], bank(f"{phase}pv{k}"), ACT.Copy).then_inc(o_copied[s].sem, 1)

            @of_batch
            def output_high(bt, phase, s):
                act.wait_ge(*o_tr[s].at(bt))
                act.wait_ge(*oh_use.before(phase, bt))
                s_.activation(halves(o_hi), bank(phase + "oT"), ACT.Copy).then_inc(ohi_done[s].sem, 1)

            @of_batch
            def gelu(bt, k):
                act.wait_ge(*f1.at(bt, k + 1))
                act.wait_ge(*h_use.before(f"T{k}", bt))
                for j in range(2):
                    s_.activation(h_f[:, k % 2, j * L:(j + 1) * L], bank(f"Tf{k}")[:, j * L:(j + 1) * L],
                                  ACT.Gelu, bias=b1_t[:, 2 * k + j:2 * k + j + 1]).then_inc(gelu_done.sem, 1)

            def finish_setup():
                act.wait_ge(gb_ready, 12)
                act.wait_ge(w_lo_ready, len(names) - 1)
                act.wait_ge(w2_lo_ready, 1)

            act.wait_ge(gb_ready, 4)
            act.wait_ge(const_ready, 5)

            def body(L_, N, A, B_, T, F):
                stacks_self(A, 0)
                stacks_self(A, 1)
                load_table(T, 0, ACT.Exp)
                stacks_self(A, 2)
                stacks_self(A, 3)
                modulate(B_, "B", "B")
                exps(T, "T", "B", 0, LC)
                exps(T, "T", "B", 1, LC)
                exps(T, "T", "B", 2, LC)
                exps(T, "T", "B", 3, LC)
                modulate(N, "N", "A")
                exps(T, "T", "B", 4, LC)
                exps(T, "T", "B", 5, LC)
                outputs(T, "T", "B", 0)
                exps(T, "T", "B", 6, LC)
                exps(T, "T", "B", 7, LC)
                outputs(T, "T", "B", 1)
                max_rows(A, "A")
                stack_high_cross(B_, 0)
                values_cross(B_)
                stack_high_cross(B_, 1)
                output_high(T, "T", "B")
                stack_high_cross(B_, 2)
                for h in range(A_EXP):
                    exps(A, "A", "A", h, P)
                    if 6 <= h < 10:
                        stack_q_cross(B_, h - 6)
                    if h == 11:
                        outputs(A, "A", "A", 0)
                    if h == 12:
                        modulate(T, "T", "C")
                load_table(T, 1, ACT.Gelu)
                max_rows(B_, "B")
                outputs(A, "A", "A", 1)
                gelu(T, 0)
                stacks_high_self(N, 0)
                gelu(T, 1)
                output_high(A, "A", "A")
                stacks_high_self(N, 1)
                gelu(T, 2)
                values_self(N)
                context_high(A)
                gelu(T, 3)
            run_turns(act, [t_use, p_use, o_use, oh_use, h_use, nat_use], body, {0: finish_setup})

        @block.vector
        def _(dve):
            v = nc.vector
            def high_half(name, ready):
                v.tensor_copy(w_hi[:, columns(name)], stage[name]).then_inc(w_hi_ready, 1)
                dve.wait_ge(w_hi_ready, ready)

            def low_half(name):
                v.tensor_tensor(w_lo[:, columns(name)], stage[name], w_hi[:, columns(name)].bitcast(f32),
                                ALU.subtract).then_inc(w_lo_ready, 1)

            def gamma_beta(norms, products):
                dve.wait_ge(gb_product, products)
                for m in (4 * k + j for k in norms for j in range(4)):
                    v.tensor_scalar(gb[:, m // 4, m % 4, :], gb_bank[:, m * B:(m + 1) * B], lnb_t[:, m:m + 1],
                                    1.0 if m % 4 < NC else 0.0, ALU.add, ALU.add).then_inc(gb_ready, 1)

            def convert_w1():
                dve.wait_ge(ld_w1, 16)
                high_half("w1", 2)
                low_half("w1")

            def finish_setup():
                dve.wait_ge(ld_rest, 16 * 7)
                high_half("w2", 3)
                gamma_beta((1, 2), 2)
                for k, name in enumerate(("sa", "q", "kv", "ca")):
                    high_half(name, k + 4)
                    low_half(name)
                dve.wait_ge(gb_ready, 12)

            gamma_beta((0,), 1)
            dve.wait_ge(ld_qkv, 16)
            high_half("qkv", 1)
            low_half("qkv")
            dve.wait_ge(gb_ready, 4)

            rot_use = Reuse(HELD, [("B0", 0, nlo_done["B"], 2), ("B1", 1, nlo_done["B"], 3),
                                   ("N0", 0, nlo_done["A"], 2), ("N1", 1, nlo_done["A"], 4)])
            rots_use = Reuse(HELD, [("B0", 0, rot_done["B"], 4), ("B1", 0, rot_done["B"], 6),
                                    ("N0", 0, rot_done["A"], 2), ("N1", 0, rot_done["A"], 4)])
            on_use = Reuse(HELD, [("T", 0, o_tr["B"], 1), ("A", 0, o_tr["A"], 1)])
            ol_use = Reuse(HELD, [("T", 0, proj_out["B"], 1), ("A", 0, proj_out["A"], 1)])
            xn_use = Reuse(HELD, [("L", 0, ln_t["A"], 1), ("T", 1, ln_t["C"], 1), ("A", 1, ln_t["B"], 1)])
            nat_use = Reuse(HELD, [("B", 0, st_t["B"], B_STACKS), ("N", 0, st_t["A"], A_STACKS)])
            norm_used = {"A": a_proj, "B": b_q, "C": f1}

            @of_batch
            def split_high(bt, s):
                dve.wait_ge(*t_done[s].at(bt))
                dve.wait_ge(*norm_used[s].at(bt + -1))
                v.tensor_copy(t_hi[s][:], t_f[:]).then_inc(thi_done[s].sem, 1)

            @of_batch
            def split_low(bt, s):
                dve.wait_ge(*thi_done[s].at(bt))
                v.tensor_tensor(t_lo[s][:], t_f[:], t_hi[s][:].bitcast(f32), ALU.subtract)\
                    .then_inc(tlo_done[s].sem, 1)

            @of_batch
            def context_low(bt):
                dve.wait_ge(*ctx_hi.at(bt))
                dve.wait_ge(*b_kv.at(bt + -1))
                v.tensor_tensor(halves(c_lo), bank("ActxT")[:, 0:NC * LC], halves(c_hi).bitcast(f32), ALU.subtract)\
                    .then_inc(ctx_lo.sem, 1)

            def rotation(s, bt, k, src, cos_out, sin_out, t, rows):
                n = src.shape[-1] // DH
                cosv = rope_t[0:rows, t, None, 0:1, :].to_broadcast([rows, n, 2, 8])
                sinv = rope_t[0:rows, t, None, 1:3, :].to_broadcast([rows, n, 2, 8])
                sv = src.rearrange("p (h s d) -> p h s d", s=2, d=8)
                cv = cos_out.rearrange("p (h s d) -> p h s d", s=2, d=8)
                ov = sin_out.rearrange("p (h s d) -> p h s d", s=2, d=8)
                v.tensor_tensor(cv, sv, cosv, ALU.mult).then_inc(cos_done[s].sem, 1)
                v.tensor_tensor(ov, sv, sinv, ALU.mult).then_inc(sin_done[s].sem, 1)
                dve.wait_ge(*sin_done[s].at(bt, k + 1))
                for half in range(2):
                    v.tensor_tensor(cv[:, :, half, :], cv[:, :, half, :], ov[:, :, 1 - half, :], ALU.add)\
                        .then_inc(rot_done[s].sem, 1)

            @of_batch
            def rotate_self(bt, t):
                dve.wait_ge(*a_proj.at(bt, t + 1))
                dve.wait_ge(*rot_use.before(f"N{t}", bt))
                dve.wait_ge(*rots_use.before(f"N{t}", bt))
                rotation("A", bt, t, bank(f"Nqk{t}"), rot_c[:, t, :], rot_s[:, :], t, P)

            @of_batch
            def rotate_cross_k(bt):
                dve.wait_ge(*b_kv.at(bt))
                rotation("B", bt, 0, bank("Bkv")[0:LC, 0:D], rk_c[:, :], rk_s[:, :], 0, LC)

            @of_batch
            def rotate_cross_q(bt, t):
                if t == 0:
                    dve.wait_ge(*b_q.at(bt))
                dve.wait_ge(*rot_use.before(f"B{t}", bt))
                dve.wait_ge(*rots_use.before(f"B{t}", bt))
                rotation("B", bt, t + 1, bank("Bq")[:, t * D:(t + 1) * D], rot_c[:, t, 0:D], rot_s[:, 0:D], t, P)

            def stack_low(s, bt, k, src, dst, block):
                dve.wait_ge(*nhi_done[s].at(bt, k + 1))
                v.tensor_tensor(dst[:, :, block * DH:(block + 1) * DH], src.rearrange("p (h d) -> p h d", d=DH),
                                dst[:, :, 0:DH].bitcast(f32), ALU.subtract).then_inc(nlo_done[s].sem, 1)

            @of_batch
            def stacks_low_self(bt, t):
                if t == 0:
                    dve.wait_ge(*nat_use.before("N", bt))
                stack_low("A", bt, 2 * t, rot_c[:, t, 0:D], q_nat[:, t], 1)
                stack_low("A", bt, 2 * t + 1, rot_c[:, t, D:2 * D], k_nat[:, t], 2)

            @of_batch
            def stack_low_cross(bt, k):
                if k == 0:
                    dve.wait_ge(*nat_use.before("B", bt))
                    stack_low("B", bt, 0, rk_c[:, :], k_nat[0:LC, 0], 2)
                else:
                    stack_low("B", bt, k, rot_c[:, k - 1, 0:D], q_nat[:, k - 1], 1)

            @of_batch
            def stack_k_cross(bt, k):
                dve.wait_ge(*st_t["B"].at(bt, k + 1))
                if k == 0:
                    dve.wait_ge(*shifted["B"].at(bt + -1))
                for par in range(2):
                    r = slice(SROW * par, SROW * (par + 1))
                    v.tensor_copy(k_st_b[r, 4 * k:4 * k + 4, par, 0:LC],
                                  bank(f"Bkst{k}")[r, :].rearrange("p (a n) -> p a n", a=4)[:, :, 0:LC])\
                        .then_inc(kst_done["B"].sem, 1)

            @of_batch
            def statistics(bt, s, src, ready):
                dve.wait_ge(*ready.at(bt))
                for t in range(NT):
                    v.bn_stats(stats[s][:, t, :], src[:, t, :]).then_inc(stat_done[s].sem, 1)

            @of_batch
            def variance(bt, s):
                dve.wait_ge(*stat_done[s].at(bt))
                v.memset(fence[s][:], 0.0)
                for t in range(NT):
                    v.bn_aggr(mv[s][:, t, :], stats[s][:, t, :]).then_inc(mv_done[s].sem, 1)
                dve.wait_ge(*mv_done[s].at(bt))
                dve.wait_ge(*rstd_done[s].at(bt + -1))
                v.tensor_scalar(ve[s][:], mv[s][:, :, 1], EPS, None, ALU.add).then_inc(var_done[s].sem, 1)

            @of_batch
            def normalise(bt, phase, s, src):
                dve.wait_ge(*rstd_done[s].at(bt))
                dve.wait_ge(*xn_use.before(phase, bt))
                for t in range(NT):
                    v.tensor_scalar(xn[s][:, t, :], src[:, t, :], mv[s][:, t, 0:1], rstd[s][:, t:t + 1],
                                    ALU.subtract, ALU.mult).then_inc(xn_done[s].sem, 1)

            @of_batch
            def maxima_self(bt, k):
                t, pair, par = k // NPAIR, 2 * (k % NPAIR // 2), k % 2
                dve.wait_ge(*score["A"].at(bt, k + 1))
                if k == 0:
                    dve.wait_ge(*nm_done["A"].at(bt + -1))
                v.reduce_max(mx["A"][:, t, :].rearrange("p (a q) -> p q a", q=2)[:, par, pair:pair + 2],
                             bank(f"Ascore{k}").rearrange("p (a n) -> p a n", a=2), AX.X).then_inc(mx_done["A"].sem, 1)

            @of_batch
            def maxima_cross(bt, k):
                t, c = k // (NPAIR // 2), k % (NPAIR // 2)
                dve.wait_ge(*score["B"].at(bt, k + 1))
                if k == 0:
                    dve.wait_ge(*nm_done["B"].at(bt + -1))
                v.reduce_max(mx["B"][:, t, 4 * c:4 * c + 4],
                             bank(f"Bscore{k}").rearrange("p (a n) -> p a n", a=4)[:, :, 0:LC],
                             AX.X).then_inc(mx_done["B"].sem, 1)

            @of_batch
            def negate(bt, s, t):
                dve.wait_ge(*mx_done[s].at(bt, (t + 1) * MAXES[s] // NT))
                if t == 0:
                    dve.wait_ge(*m_tr[s].at(bt + -1))
                mv_ = mx[s][:, t, :].rearrange("p (a q) -> p q a", q=2)
                v.tensor_scalar(nm[s][:, t, :, 0, :], mv_, -1.0, None, ALU.mult).then_inc(nmhi_done[s].sem, 1)
                dve.wait_ge(*nmhi_done[s].at(bt, t + 1))
                v.scalar_tensor_tensor(out=nm[s][:, t, :, 1, :], in0=mv_, scalar=-1.0,
                                       in1=nm[s][:, t, :, 0, :].bitcast(f32), op0=ALU.mult,
                                       op1=ALU.subtract).then_inc(nm_done[s].sem, 1)

            @of_batch
            def divide(bt, phase, s, t):
                dve.wait_ge(*o_nat[s].at(bt, t + 1))
                src = bank(f"{phase}on{t}").rearrange("p (h w) -> p h w", w=VW)
                if t == 0:
                    dve.wait_ge(*on_use.before(phase, bt))
                v.reciprocal(rden[:, t, :], src[:, :, DH]).then_inc(rden_done[s].sem, 1)
                dve.wait_ge(*rden_done[s].at(bt, t + 1))
                v.tensor_tensor(o_n[:, t, :].rearrange("p (h d) -> p h d", d=DH), src[:, :, 0:DH],
                                rden[:, t, :, None].to_broadcast([P, H, DH]), ALU.mult).then_inc(on_done[s].sem, 1)

            @of_batch
            def output_low(bt, phase, s):
                dve.wait_ge(*ohi_done[s].at(bt))
                dve.wait_ge(*ol_use.before(phase, bt))
                v.tensor_tensor(halves(o_lo), bank(phase + "oT"), halves(o_hi).bitcast(f32), ALU.subtract)\
                    .then_inc(olo_done[s].sem, 1)

            @of_batch
            def residual(bt, phase, s, acc, there):
                dve.wait_ge(*proj_out[s].at(bt))
                dve.wait_ge(*there.at(bt))
                v.tensor_tensor(halves(acc), bank(phase + "out"), halves(acc), ALU.add).then_inc(res_done[s].sem, 1)

            @of_batch
            def gelu_high(bt, k):
                dve.wait_ge(*gelu_done.at(bt, 2 * k + 2))
                if k == 0:
                    dve.wait_ge(*proj_out["C"].at(bt + -1))
                v.tensor_copy(h_hi[:, 2 * k:2 * k + 2, :],
                              h_f[:, k % 2, :].rearrange("p (c n) -> p c n", c=2)).then_inc(hhi_done.sem, 1)

            def body(L_, N, A, B_, T, F):
                for k in range(A_MAX):
                    maxima_self(A, k)
                    if k == 5:
                        split_high(B_, "B")
                    if k == 6:
                        split_low(B_, "B")
                    if k == 11:
                        split_high(N, "A")
                    if k == 12:
                        split_low(N, "A")
                    if k == NPAIR - 1:
                        negate(A, "A", 0)
                negate(A, "A", 1)
                rotate_cross_k(B_)
                divide(T, "T", "B", 0)
                divide(T, "T", "B", 1)
                rotate_cross_q(B_, 0)
                rotate_cross_q(B_, 1)
                output_low(T, "T", "B")
                for k in range(NT + 1):
                    stack_low_cross(B_, k)
                residual(F, "F", "C", xc, xc_made)
                residual(T, "T", "B", xt, xt_copied)
                statistics(T, "C", xt, res_done["B"])
                stack_k_cross(B_, 0)
                stack_k_cross(B_, 1)
                variance(T, "C")
                statistics(L_, "A", x_in, x_loaded)
                normalise(T, "T", "C", xt)
                variance(L_, "A")
                for k in range(B_MAX):
                    maxima_cross(B_, k)
                    if k == 3:
                        normalise(L_, "L", "A", x_in)
                    if k % (NPAIR // 2) == NPAIR // 2 - 1:
                        negate(B_, "B", k // (NPAIR // 2))
                split_high(T, "C")
                split_low(T, "C")
                rotate_self(N, 0)
                divide(A, "A", "A", 0)
                divide(A, "A", "A", 1)
                rotate_self(N, 1)
                gelu_high(T, 0)
                output_low(A, "A", "A")
                stacks_low_self(N, 0)
                gelu_high(T, 1)
                stacks_low_self(N, 1)
                context_low(A)
                residual(A, "A", "A", xa, xa_loaded)
                statistics(A, "B", xa, res_done["A"])
                variance(A, "B")
                gelu_high(T, 2)
                normalise(A, "A", "B", xa)
                gelu_high(T, 3)
            run_turns(dve, [rot_use, rots_use, on_use, ol_use, xn_use, nat_use], body,
                      {-1: convert_w1, 0: finish_setup})

        @block.tensor
        def _(pe):
            mm, tr = nc.tensor.matmul, nc.tensor.transpose
            wqkv_, wsa_, wq_, wkv_, wca_, w1_ = (weight(n, NC) for n in ("qkv", "sa", "q", "kv", "ca", "w1"))
            w2_ = weight("w2", NF)
            bank_use = Reuse(HELD, bank_uses)

            def fill(name, bt):
                pe.wait_ge(*bank_use.before(name, bt))
                return bank(name)

            def split_product(out_, terms):
                n = len(terms)
                for k, (l, r) in enumerate(terms):
                    last = mm(out_, l, r, start=(k == 0), stop=(k == n - 1))
                return last

            def three(xh, xl, w, xs, ws):
                wh, wl = w
                return [(x_[:, c, xs], w_[:, c, ws]) for c in range(NC) for x_, w_ in ((xh, wh), (xl, wh), (xh, wl))]

            def by_tiles(o, xh, xl, w, ws):
                for t in range(NT):
                    last = split_product(o[:, t * D:(t + 1) * D], three(xh, xl, w, slice(t * P, (t + 1) * P), ws))
                return last

            @of_batch
            def norm_transpose(bt, phase, s):
                pe.wait_ge(*xn_done[s].at(bt))
                o = fill(phase + "lnT", bt)
                for c in range(NC):
                    for t in range(NT):
                        last = tr(o[:, c * L + t * P:c * L + (t + 1) * P], xn[s][:, t, c * P:(c + 1) * P], ident[:])
                last.then_inc(ln_t[s].sem, 1)

            @of_batch
            def context_transpose(bt):
                pe.wait_ge(*ctx_loaded.at(bt))
                o = fill("ActxT", bt)
                for c in range(NC):
                    last = tr(o[:, c * LC:(c + 1) * LC], ctx_in[:, c * P:(c + 1) * P], ident[0:LC, 0:LC])
                last.then_inc(ctx_t.sem, 1)

            @of_batch
            def project_qk(bt, t):
                if t == 0:
                    pe.wait_ge(*tlo_done["A"].at(bt))
                o = fill(f"Nqk{t}", bt)
                split_product(o, three(t_hi["A"], t_lo["A"], wqkv_, slice(t * P, (t + 1) * P), slice(0, 2 * D)))\
                    .then_inc(a_proj.sem, 1)

            @of_batch
            def project_v(bt):
                o = fill("Nv", bt)
                by_tiles(o, t_hi["A"], t_lo["A"], wqkv_, slice(2 * D, 3 * D)).then_inc(a_proj.sem, 1)

            @of_batch
            def project_context(bt):
                pe.wait_ge(*ctx_lo.at(bt))
                o = fill("Bkv", bt)
                split_product(o[0:LC, :], three(c_hi, c_lo, wkv_, slice(0, LC), slice(0, 2 * D))).then_inc(b_kv.sem, 1)

            @of_batch
            def project_q(bt):
                pe.wait_ge(*tlo_done["B"].at(bt))
                o = fill("Bq", bt)
                by_tiles(o, t_hi["B"], t_lo["B"], wq_, slice(0, D)).then_inc(b_q.sem, 1)

            def stack_transposes(o, jobs):
                for col, src, rows in jobs:
                    last = tr(o[:, col:col + rows].bitcast(f32r), src, ident_r[0:rows, 0:rows])
                return last

            def pair_of(nat_, t, p, rows=P):
                return nat_[0:rows, t, 2 * p:2 * p + 2, :].rearrange("p h w -> p (h w)")

            @of_batch
            def stacks_self(bt, k):
                if k == 0:
                    pe.wait_ge(*nlo_done["A"].at(bt))
                for name, nat_ in (("Aqst", q_nat), ("Akst", k_nat)):
                    o = fill(f"{name}{k}", bt)
                    stack_transposes(o, [(a * L + t * P, pair_of(nat_, t, 2 * k + a), P)
                                         for a in range(2) for t in range(NT)]).then_inc(st_t["A"].sem, 1)

            @of_batch
            def stacks_cross_q(bt, k):
                if k == 0:
                    pe.wait_ge(*nlo_done["B"].at(bt))
                o = fill(f"Bqst{k}", bt)
                stack_transposes(o, [(a * L + t * P, pair_of(q_nat, t, 2 * k + a), P)
                                     for a in range(2) for t in range(NT)]).then_inc(st_t["B"].sem, 1)

            @of_batch
            def stacks_cross_k(bt, k):
                if k == 0:
                    pe.wait_ge(*nlo_done["B"].at(bt, 1))
                o = fill(f"Bkst{k}", bt)
                stack_transposes(o, [(a * P, pair_of(k_nat, 0, 4 * k + a, LCE), LCE) for a in range(4)])\
                    .then_inc(st_t["B"].sem, 1)

            @of_batch
            def max_transpose(bt, s):
                pe.wait_ge(*nm_done[s].at(bt))
                o = fill(s + "mT", bt)
                for t in range(NT):
                    last = tr(o[0:2 * H, t * P:(t + 1) * P].bitcast(f32r),
                              nm[s][:, t].rearrange("p q j a -> p (q j a)"), ident_r[:])
                last.then_inc(m_tr[s].sem, 1)

            @of_batch
            def scores_self(bt, k):
                t, pair, par = k // NPAIR, 2 * (k % NPAIR // 2), k % 2
                if t == 0 and par == 0:
                    pe.wait_ge(*qst_done["A"].at(bt, k // 2 + 1))
                    pe.wait_ge(*kst_done["A"].at(bt, k // 2 + 1))
                o = fill(f"Ascore{k}", bt)
                r = slice(SROW * par, SROW * par + NS)
                for j in range(2):
                    last = mm(o[:, j * L:(j + 1) * L], q_st["A"][r, pair + j, t * P:(t + 1) * P],
                              k_st_a[r, pair + j, :], start=True, stop=True)
                last.then_inc(score["A"].sem, 1)

            @of_batch
            def scores_cross(bt, k):
                t, c = k // (NPAIR // 2), k % (NPAIR // 2)
                if t == 0:
                    pe.wait_ge(*qst_done["B"].at(bt, k + 1))
                    pe.wait_ge(*kst_done["B"].at(bt, 2 * (k // 2) + 2))
                o = fill(f"Bscore{k}", bt)
                for j in range(2):
                    last = mm(o[:, j * L:(j + 1) * L], q_st["B"][:, 2 * c + j, t * P:(t + 1) * P],
                              k_st_b[:, 2 * c + j].rearrange("p q n -> p (q n)"), start=True, stop=True)
                last.then_inc(score["B"].sem, 1)

            @of_batch
            def shifted_self(bt, h):
                if h == 0:
                    pe.wait_ge(*m_rows["A"].at(bt))
                o, pair = fill(f"Ashift{h}", bt), h // 2
                r = slice(SROW * (h % 2), SROW * (h % 2) + NSM)
                for t in range(NT):
                    last = mm(o[:, t * L:(t + 1) * L], k_st_a[r, pair, t * P:(t + 1) * P], q_st["A"][r, pair, :],
                              start=True, stop=True)
                last.then_inc(shifted["A"].sem, 1)

            @of_batch
            def shifted_cross(bt, pair):
                if pair == 0:
                    pe.wait_ge(*m_rows["B"].at(bt))
                o = fill(f"Tshift{pair}", bt)
                for par in range(2):
                    last = mm(o[0:LC, par * L:(par + 1) * L], k_st_b[:, pair, par, 0:LC], q_st["B"][:, pair, :],
                              start=True, stop=True)
                last.then_inc(shifted["B"].sem, 1)

            @of_batch
            def weighted(bt, phase, s, g_):
                pe.wait_ge(*p_done[s].at(bt, (g_ + 1) * EXPS[s] // NG))
                if g_ == 0:
                    pe.wait_ge(*v_ready[s].at(bt))
                name = f"{phase}pv{g_ // 2}"
                o = (fill(name, bt) if g_ % 2 == 0 else bank(name))[:, (g_ % 2) * L:(g_ % 2 + 1) * L]
                for t in range(NT if s == "A" else 1):
                    for j in range(GRP):
                        h = GRP * g_ + j
                        if s == "A":
                            l, r = v_a[:, t, h, :], probs[:, h % NSLOT, t * L:(t + 1) * L]
                        else:
                            l, r = v_b[:, h, :], probs[0:LC, h // 2, (h % 2) * L:(h % 2 + 1) * L]
                        last = mm(o[VW * j:VW * (j + 1), :], l, r, start=(t == 0),
                                  stop=(s == "B" or t == NT - 1))
                last.then_inc(pv[s].sem, 1)

            @of_batch
            def output_natural(bt, phase, s):
                pe.wait_ge(*o_copied[s].at(bt))
                for t in range(NT):
                    o = fill(f"{phase}on{t}", bt)
                    for g_ in range(NG):
                        last = tr(o[:, g_ * P:(g_ + 1) * P],
                                  o_st[:, g_ // 2, (g_ % 2) * L + t * P:(g_ % 2) * L + (t + 1) * P], ident[:])
                    last.then_inc(o_nat[s].sem, 1)

            @of_batch
            def output_transpose(bt, phase, s):
                pe.wait_ge(*on_done[s].at(bt))
                o = fill(phase + "oT", bt)
                for c in range(NC):
                    for t in range(NT):
                        last = tr(o[:, c * L + t * P:c * L + (t + 1) * P], o_n[:, t, c * P:(c + 1) * P], ident[:])
                last.then_inc(o_tr[s].sem, 1)

            @of_batch
            def output_product(bt, phase, s):
                pe.wait_ge(*olo_done[s].at(bt))
                o = fill(phase + "out", bt)
                by_tiles(o, o_hi, o_lo, wsa_ if s == "A" else wca_, slice(0, D)).then_inc(proj_out[s].sem, 1)

            @of_batch
            def hidden(bt, k):
                if k == 0:
                    pe.wait_ge(*tlo_done["C"].at(bt))
                o = fill(f"Tf{k}", bt)
                for j in range(2):
                    f = slice((2 * k + j) * P, (2 * k + j + 1) * P)
                    last = split_product(o[:, j * L:(j + 1) * L],
                                         [(w_[:, c, f], x_[:, c, :]) for c in range(NC)
                                          for w_, x_ in ((w1_[0], t_hi["C"]), (w1_[0], t_lo["C"]),
                                                         (w1_[1], t_hi["C"]))])
                last.then_inc(f1.sem, 1)

            @of_batch
            def feed_forward_out(bt, part):
                o = fill("Fout", bt) if part == 0 else bank("Fout")
                per_tile = A_MAX // NT
                t, f = part // per_tile, part % per_tile
                if t == 0 and f % 2 == 0:
                    pe.wait_ge(*hlo_done.at(bt, f // 2 + 1))
                for n, (h_, w_) in enumerate(((h_hi, w2_[0]), (h_lo, w2_[0]), (h_hi, w2_[1]))):
                    last = mm(o[:, t * D:(t + 1) * D], h_[:, f, t * P:(t + 1) * P], w_[:, f, :],
                              start=(f == 0 and n == 0), stop=(f == NF - 1 and n == 2))
                if part == A_MAX - 1:
                    last.then_inc(proj_out["C"].sem, 1)

            def gamma_beta(norms):
                for m in (4 * k + j for k in norms for j in range(4)):
                    for c in range(NC):
                        last = mm(gb_bank[:, m * B:(m + 1) * B], lnw_stage(m // 4)[:, c, (m % 4) * P:(m % 4 + 1) * P],
                                  cond_s[:, c, :], start=(c == 0), stop=(c == NC - 1))
                last.then_inc(gb_product, 1)

            def other_norms():
                pe.wait_ge(ld_norms, 16 * 2)
                gamma_beta((1, 2))

            def finish_setup():
                pe.wait_ge(ld_rest, 16 * 7)
                pe.wait_ge(gb_ready, 12)
                pe.wait_ge(w_lo_ready, len(names) - 1)
                pe.wait_ge(w2_lo_ready, 1)

            pe.wait_ge(ld_first, 16 * 4)
            gamma_beta((0,))
            pe.wait_ge(gb_ready, 4)
            pe.wait_ge(const_ready, 5)
            pe.wait_ge(w_lo_ready, 1)

            def body(L_, N, A, B_, T, F):
                stacks_self(A, 0)
                feed_forward_out(F, 0)
                feed_forward_out(F, 1)
                stacks_self(A, 1)
                feed_forward_out(F, 2)
                for k in range(A_MAX):
                    scores_self(A, k)
                    if k % 2 == 1 and k < 15:
                        feed_forward_out(F, k // 2 + 3)
                    if k == 1:
                        stacks_self(A, 2)
                        norm_transpose(B_, "B", "B")
                    if k == 3:
                        stacks_self(A, 3)
                    if 5 <= k < 5 + B_EXP:
                        shifted_cross(T, k - 5)
                    if k == 9:
                        norm_transpose(N, "N", "A")
                    if k >= 8 and k % 2 == 0:
                        weighted(T, "T", "B", (k - 8) // 2)
                    if k == 15:
                        project_context(B_)
                feed_forward_out(F, 10)
                max_transpose(A, "A")
                output_natural(T, "T", "B")
                project_q(B_)
                output_transpose(T, "T", "B")
                for part in range(11, 14):
                    feed_forward_out(F, part)
                for h in range(A_EXP):
                    shifted_self(A, h)
                    if h == 1:
                        feed_forward_out(F, 14)
                        feed_forward_out(F, 15)
                        project_qk(N, 0)
                    if h == 2:
                        output_product(T, "T", "B")
                    if h % GRP == 1 and h > GRP:
                        weighted(A, "A", "A", h // GRP - 1)
                    if h == 4:
                        stacks_cross_k(B_, 0)
                        stacks_cross_k(B_, 1)
                    if 6 <= h < 10:
                        stacks_cross_q(B_, h - 6)
                    if 10 <= h < 14:
                        scores_cross(B_, 2 * (h - 10))
                        scores_cross(B_, 2 * (h - 10) + 1)
                    if h == 10:
                        norm_transpose(T, "T", "C")
                    if h == 15:
                        project_qk(N, 1)
                max_transpose(B_, "B")
                weighted(A, "A", "A", NG - 1)
                hidden(T, 0)
                output_natural(A, "A", "A")
                hidden(T, 1)
                output_transpose(A, "A", "A")
                project_v(N)
                context_transpose(A)
                hidden(T, 2)
                output_product(A, "A", "A")
                hidden(T, 3)
            run_turns(pe, [bank_use], body, {-1: other_norms, 0: finish_setup})


_OUT = ((B, L, D), "float32")


def kernel(**inputs):
    import numpy as np
    import concourse.bacc as bacc
    from concourse.bass_utils import run_bass_kernel_spmd

    f = {k: np.asarray(v) for k, v in inputs.items()}
    w = {k[len("L0_xcond_"):]: v for k, v in f.items() if k.startswith("L0_xcond_")}
    half = DH // 2
    inv_freq = (np.float32(1.0) / np.float32(10000.0) ** (np.arange(half, dtype=np.float32) / np.float32(half)))
    ang = np.arange(L, dtype=np.float32)[:, None] * inv_freq.astype(np.float32)[None, :]
    rope = np.concatenate([np.cos(ang), np.sin(ang), -np.sin(ang)], axis=1).astype(np.float32)
    arrays = {
        "x": f["x"], "ctx": f["ctx_1024"], "cond_t": f["cond_1024"].T, "rope": rope,
        "wqkv": w["qkv_w"].T, "wsa": w["sa_out_w"].T, "wq": w["q_w"].T,
        "wkv": np.concatenate([w["k_w"].T, w["v_w"].T], axis=1), "wca": w["ca_out_w"].T,
        "w1": w["ffn_w1"].T, "w2": w["ffn_w2"].T,
        "lnw": np.stack([w[f"ln{k}_w"].T for k in (1, 2, 3)]),
        "lnb": np.concatenate([w[f"ln{k}_b"].reshape(4, P).T for k in (1, 2, 3)], axis=1),
        "b1": w["ffn_b1"].reshape(NF, P).T, "b2": w["ffn_b2"],
    }
    nc = bacc.Bacc("TRN2", target_bir_lowering=False, num_devices=1)
    host, args = {}, []
    for name, a in arrays.items():
        a = np.ascontiguousarray(a)
        host[f"in_{name}"] = a
        args.append(nc.dram_tensor(f"in_{name}", a.shape, mybir.dt.from_np(a.dtype), kind="ExternalInput").ap())
    args.append(nc.dram_tensor("out_x", _OUT[0], mybir.dt.float32, kind="ExternalOutput").ap())
    layer_kernel(nc, *args)
    r = run_bass_kernel_spmd(nc, [host], core_ids=[0])
    return r.results[0]["out_x"]
```
